# Optimizing a Trainium2 kernel written in Bass

```python
import numpy as np
import jax
import jax.numpy as jnp

def _softmax(x, axis=-1):
    return jax.nn.softmax(x, axis=axis)

def _gelu(x):
    return jax.nn.gelu(x, approximate=True)

def _silu(x):
    return jax.nn.silu(x)

def _sigmoid(x):
    return jax.nn.sigmoid(x)

def _layernorm(x, axis=-1, eps=1e-05):
    m = jnp.mean(x, axis=axis, keepdims=True)
    v = jnp.var(x, axis=axis, keepdims=True)
    return (x - m) / jnp.sqrt(v + eps)

def _scatter_add(tgt, idx, src, axis=0):
    return tgt.at[idx].add(src)

def _segment_sum(src, seg, n):
    return jax.ops.segment_sum(src, seg, n)
kernel_name = 'mk_metaformer_d1_conv_nchw128_r2_715e45'

def setup_inputs(seed: int=0):
    np.random.seed(seed)
    _w = jnp.asarray

    def _rec_inputs():
        import jax
        import jax.numpy as jnp
        _gk = jax.random.key(seed)
        x = -9.26e-05 + 0.9999 * jax.random.normal(jax.random.fold_in(_gk, 1), (8, 64, 96, 96), jnp.float32)
        return x
    x = _rec_inputs()

    def _L0_conv_setup():
        import jax, jax.numpy as jnp
        import numpy as np
        SP = 4
        HEADS = 8
        SHIFTS = (0, 2)

        def _rel_pos_index(sp):
            coords = np.stack(np.meshgrid(np.arange(sp), np.arange(sp), indexing='ij'))
            coords = coords.reshape(2, -1)
            rel = coords[:, :, None] - coords[:, None, :]
            rel = rel.transpose(1, 2, 0).astype(np.int64)
            rel[..., 0] += sp - 1
            rel[..., 1] += sp - 1
            rel[..., 0] *= 2 * sp - 1
            return rel.sum(-1)

        def _window_attend(xh, qkv_w, lepe_w, bias, sp, heads, scale):
            B, c, H, W = xh.shape
            hd = c // heads
            h, w = (H // sp, W // sp)
            qkv = jnp.einsum('oi,bihw->bohw', qkv_w, xh)
            q, k, v = jnp.split(qkv, 3, axis=1)
            lepe = jax.lax.conv_general_dilated(v, lepe_w, (1, 1), 'SAME', feature_group_count=c)

            def part(t):
                t = t.reshape(B, hd, heads, h, sp, w, sp)
                t = t.transpose(0, 3, 5, 2, 4, 6, 1)
                return t.reshape(B * h * w, heads, sp * sp, hd)
            q, k, v, lepe = map(part, (q, k, v, lepe))
            attn = jnp.einsum('nhqc,nhkc->nhqk', q * scale, k) + bias[None]
            attn = jax.nn.softmax(attn, axis=-1)
            out = jnp.einsum('nhqk,nhkc->nhqc', attn, v) + lepe
            out = out.reshape(B, h, w, heads, sp, sp, hd)
            out = out.transpose(0, 6, 3, 1, 4, 2, 5).reshape(B, c, H, W)
            return out
        key = jax.random.key(seed)
        k1, k2, k3, k4 = jax.random.split(key, 4)
        x = jax.random.normal(k1, (8, 64, 96, 96), dtype=jnp.float32)
        qkv_w = jax.random.normal(k2, (96, 32), dtype=jnp.float32) * 0.05
        lepe_w = jax.random.normal(k3, (32, 1, 3, 3), dtype=jnp.float32) * 0.05
        bias_table = jax.random.normal(k4, (49, 8), dtype=jnp.float32) * 0.02
        return {'x': x, 'qkv_w': qkv_w, 'lepe_w': lepe_w, 'bias_table': bias_table}
    _L0_conv_all = _L0_conv_setup()
    _L0_conv_in = {k: v for k, v in _L0_conv_all.items() if k in ('qkv_w', 'lepe_w', 'bias_table')}
    del _L0_conv_all

    def _L0_ffn_setup():
        import jax, jax.numpy as jnp
        import numpy as np
        B, N, D, C, E, K = (8, 4096, 64, 64, 8, 2)
        key = jax.random.key(seed)
        k0, k1, k2 = jax.random.split(key, 3)
        x = jax.random.normal(k0, (B, N, D), dtype=jnp.float32)
        router_w = jax.random.normal(k1, (D, E), dtype=jnp.float32) * 0.05
        router_b = jnp.zeros((E,), dtype=jnp.float32)
        expert_w = jax.random.normal(k2, (E, D, C), dtype=jnp.float32) * (1.0 / np.sqrt(D))
        expert_b = jnp.zeros((E, C), dtype=jnp.float32)
        return {'x': x, 'router_w': router_w, 'router_b': router_b, 'expert_w': expert_w, 'expert_b': expert_b}
    _L0_ffn_all = _L0_ffn_setup()
    _L0_ffn_in = {k: v for k, v in _L0_ffn_all.items() if k in ('router_w', 'router_b', 'expert_w', 'expert_b')}
    del _L0_ffn_all
    return {'x': x, 'L0_conv_qkv_w': _L0_conv_in['qkv_w'], 'L0_conv_lepe_w': _L0_conv_in['lepe_w'], 'L0_conv_bias_table': _L0_conv_in['bias_table'], 'L0_ffn_router_w': _L0_ffn_in['router_w'], 'L0_ffn_router_b': _L0_ffn_in['router_b'], 'L0_ffn_expert_w': _L0_ffn_in['expert_w'], 'L0_ffn_expert_b': _L0_ffn_in['expert_b']}

def reference(x, L0_conv_qkv_w, L0_conv_lepe_w, L0_conv_bias_table, L0_ffn_router_w, L0_ffn_router_b, L0_ffn_expert_w, L0_ffn_expert_b):
    import jax
    import jax.numpy as jnp

    def _L0_conv_ref(x, qkv_w, lepe_w, bias_table):
        import jax, jax.numpy as jnp
        import numpy as np
        SP = 4
        HEADS = 8
        SHIFTS = (0, 2)

        def _rel_pos_index(sp):
            coords = np.stack(np.meshgrid(np.arange(sp), np.arange(sp), indexing='ij'))
            coords = coords.reshape(2, -1)
            rel = coords[:, :, None] - coords[:, None, :]
            rel = rel.transpose(1, 2, 0).astype(np.int64)
            rel[..., 0] += sp - 1
            rel[..., 1] += sp - 1
            rel[..., 0] *= 2 * sp - 1
            return rel.sum(-1)

        def _window_attend(xh, qkv_w, lepe_w, bias, sp, heads, scale):
            B, c, H, W = xh.shape
            hd = c // heads
            h, w = (H // sp, W // sp)
            qkv = jnp.einsum('oi,bihw->bohw', qkv_w, xh)
            q, k, v = jnp.split(qkv, 3, axis=1)
            lepe = jax.lax.conv_general_dilated(v, lepe_w, (1, 1), 'SAME', feature_group_count=c)

            def part(t):
                t = t.reshape(B, hd, heads, h, sp, w, sp)
                t = t.transpose(0, 3, 5, 2, 4, 6, 1)
                return t.reshape(B * h * w, heads, sp * sp, hd)
            q, k, v, lepe = map(part, (q, k, v, lepe))
            attn = jnp.einsum('nhqc,nhkc->nhqk', q * scale, k) + bias[None]
            attn = jax.nn.softmax(attn, axis=-1)
            out = jnp.einsum('nhqk,nhkc->nhqc', attn, v) + lepe
            out = out.reshape(B, h, w, heads, sp, sp, hd)
            out = out.transpose(0, 6, 3, 1, 4, 2, 5).reshape(B, c, H, W)
            return out
        B, C, H, W = x.shape
        c = C // 2
        hd = c // HEADS
        scale = hd ** (-0.5)
        idx = _rel_pos_index(SP)
        bias = bias_table[idx.reshape(-1)].reshape(SP * SP, SP * SP, HEADS)
        bias = bias.transpose(2, 0, 1)
        results = []
        for s in SHIFTS:
            xs = jnp.roll(x, (-s, -s), axis=(1, 2)) if s > 0 else x
            halves = (xs[:, :c], xs[:, c:])
            outs = [_window_attend(xh, qkv_w, lepe_w, bias, SP, HEADS, scale) for xh in halves]
            if s > 0:
                outs = [jnp.roll(o, (s, s), axis=(1, 2)) for o in outs]
            results.append(jnp.concatenate(outs, axis=1))
        return results[0] + results[1]

    def _L0_ffn_ref(x, router_w, router_b, expert_w, expert_b):
        import jax, jax.numpy as jnp
        import numpy as np
        B, N, D, C, E, K = (8, 4096, 64, 64, 8, 2)
        router_probs = jax.nn.softmax(x @ router_w + router_b, axis=-1)
        top_p, top_i = jax.lax.top_k(router_probs, K)
        top_p = top_p / jnp.sum(top_p, axis=-1, keepdims=True)
        expert_out = jnp.einsum('bnd,edc->bnec', x, expert_w) + expert_b
        gathered = jnp.take_along_axis(expert_out, top_i[..., None], axis=2)
        return jnp.einsum('bnk,bnkc->bnc', top_p, gathered)

    def _gn(v, G=32, eps=1e-05):
        B_, C_, H_, W_ = v.shape
        g = v.reshape(B_, G, C_ // G, H_, W_)
        m = jnp.mean(g, axis=(2, 3, 4), keepdims=True)
        s = jnp.var(g, axis=(2, 3, 4), keepdims=True)
        return ((g - m) / jnp.sqrt(s + eps)).reshape(v.shape)

    def _ln_c(v, eps=1e-06):
        m = jnp.mean(v, axis=1, keepdims=True)
        s = jnp.var(v, axis=1, keepdims=True)
        return (v - m) / jnp.sqrt(s + eps)

    def _ln_t(v, eps=1e-05):
        m = jnp.mean(v, axis=-1, keepdims=True)
        s = jnp.var(v, axis=-1, keepdims=True)
        return (v - m) / jnp.sqrt(s + eps)

    def _to_tokens(v):
        B_, C_, H_, W_ = v.shape
        return v.reshape(B_, C_, H_ * W_).transpose(0, 2, 1)

    def _from_tokens(t, like):
        B_, C_, H_, W_ = like.shape
        return t.transpose(0, 2, 1).reshape(B_, C_, H_, W_)
    x = x + _L0_conv_ref(_ln_c(x), L0_conv_qkv_w, L0_conv_lepe_w, L0_conv_bias_table)
    t = _to_tokens(x)
    t = t + _L0_ffn_ref(_ln_t(t), L0_ffn_router_w, L0_ffn_router_b, L0_ffn_expert_w, L0_ffn_expert_b)
    x = _from_tokens(t, x)
    return x

_drawn_inputs = setup_inputs


def setup_inputs(seed=0):
    import zlib

    import numpy as np

    out = dict(_drawn_inputs(seed))
    spreads = {'L0_ffn_router_b': (0.0, 0.1), 'L0_ffn_expert_b': (0.0, 0.1)}
    factors = {'L0_conv_bias_table': 2.965}
    for name, (base, spread) in spreads.items():
        noise = np.random.default_rng([zlib.crc32(name.encode()), seed]).standard_normal(out[name].shape)
        drawn = base * np.exp(spread * noise) if base else spread * noise
        out[name] = jnp.asarray(drawn.astype(out[name].dtype))
    for name, factor in factors.items():
        out[name] = (out[name] * factor).astype(out[name].dtype)
    return out
```

```python
from contextlib import ExitStack

import numpy as np
import concourse.bass as bass
from concourse import mybir

FP32 = mybir.dt.float32
BF16 = mybir.dt.bfloat16
ALU = mybir.AluOpType
ACT = mybir.ActivationFunctionType
AX = mybir.AxisListType

B, C, H, W = 8, 64, 96, 96
CH = C // 2
HEADS, HD = 8, 4
SP = 4
TOK = SP * SP
E = 8
ROLL = 2
STRIPS = H // SP
SPX = SP * W
UW = 8
UNITS = W // SP // UW
UPX = UW * TOK
IMU = STRIPS * UNITS
KEYS = 4 * TOK
UK = UW * KEYS
PADW = W + 2
HALFH = H // 2
TILES = HALFH // SP
TBLK = SPX // 128
GATES = TILES * TBLK * 2
LN1_EPS, LN2_EPS = 1e-6, 1e-5



def _constants():
    p = np.arange(128)
    g, c = p // CH, p % CH
    head = c % HEADS
    same64 = (p[:, None] // C == p[None, :] // C).astype(np.float32)
    parts = {
        "ident": np.eye(128),
        "center": np.eye(128) - same64 / C,
        "mean": same64 / C,
        "mask_q": (g[:, None] == p[None, :8] // 2) & ((head >> 2)[:, None] == p[None, :8] % 2),
        "mask_k": (head & 3)[:, None] == p[None, :4],
        "mask_v": (g[:, None] == p[None, :8] // 2) & ((head & 1)[:, None] == p[None, :8] % 2),
        "mask_o": (((head >> 1) & 1)[:, None] == p[None, :4] // 2) & ((head >> 2)[:, None] == p[None, :4] % 2),
        "ident64x2": np.concatenate([np.eye(64), np.eye(64)]),
        "expert_sel": np.stack([(p[:, None] % E == e) & (p[:, None] // E == p[None, :] // C)
                                for e in range(E)], axis=1).reshape(128, E * 128),
        "mask_b": (p[:, None] // TOK % 4) == p[None, :4],
        "rank": np.tile(E - np.arange(E), (128, 1)),
        "eps1": np.full((128, 1), LN1_EPS),
        "eps2": np.full((128, 1), LN2_EPS),
    }
    at, cols = {}, 0
    for name, a in parts.items():
        at[name] = (cols, a.shape[1])
        cols += a.shape[1]
    return at, np.concatenate([a.astype(np.float32) for a in parts.values()], axis=1)


CONST_AT, CONSTS = _constants()


def metaformer_block(nc, x, qkv_w, lepe_w, bias_table, router_w, router_b, expert_w, expert_b, consts, out):
    ctx = ExitStack()
    with ctx:
        def sb(name, shape, dt=FP32):
            return ctx.enter_context(nc.sbuf_tensor(name, shape, dt))

        def sem(name):
            return ctx.enter_context(nc.semaphore(name))

        z = nc.dram_tensor("z", [2, B, C, H, W], FP32, kind="Internal").ap()

        const_sb = sb("const_sb", [128, CONSTS.shape[1]])

        def const(name, rows=128):
            at, n = CONST_AT[name]
            return const_sb[0:rows, at:at + n]

        wqkv = sb("wqkv", [128, 3, 128])
        lepe_sb = sb("lepe_sb", [128, 9])
        bias_all = sb("bias_all", [128, TOK, HEADS])
        bias_sb = sb("bias_sb", [128, 2 * TOK])
        bias_rest = sb("bias_rest", [128, 2, 2 * TOK])
        bias_part = sb("bias_part", [128, 3, 2 * TOK], BF16)
        bias_hi_mid = sb("bias_hi_mid", [128, 128], BF16)
        bias_lo = sb("bias_lo", [64, 128], BF16)
        key_sel = sb("key_sel", [128, UK], BF16)
        router_sb = sb("router_sb", [128, 2 * E])
        router_bias = sb("router_bias", [2 * E, 1])
        expert_sb = sb("expert_sb", [128, E, 128])
        expert_bias = sb("expert_bias", [2 * E, 128])

        xs = sb("xs", [128, H * W])
        vpad = sb("vpad", [128, (H + 2) * PADW])
        y = sb("y", [128, HALFH * W])
        z0 = sb("z0", [128, HALFH * W])
        z2 = sb("z2", [128, HALFH * W])
        yn = z0
        assert 7 * GATES * E + 4 * GATES <= HALFH * W

        def gate_buf(n):
            return z2[:, n * GATES * E:(n + 1) * GATES * E]

        def gate_vec(n):
            at = 7 * GATES * E + n * GATES
            return z2[:, at:at + GATES]

        logitT = sb("logitT", [2 * E, 2, SPX])
        logits = sb("logits", [128, GATES * E])
        q_sb = sb("q_sb", [128, 2, SPX])
        k_sb = sb("k_sb", [128, 2, SPX])
        v_sb = sb("v_sb", [128, 2, SPX])
        sq, rstd = q_sb, k_sb
        qx = sb("qx", [128, 2, UW, 128])
        kx = sb("kx", [128, 2, UW, KEYS])
        vx = sb("vx", [128, 2, UW, 128])
        vt = sb("vt", [128, 2, UW, 128])
        prob = sb("prob", [128, 2, UK])
        probT = sb("probT", [128, 2, UW, KEYS])
        row_max = sb("row_max", [128, 2, UW * 4])
        row_sum = sb("row_sum", [128, 2, UW * 4])
        row_inv = sb("row_inv", [128, 2, UW * 4])
        att = sb("att", [128, 2, SPX])
        lepe = sb("lepe", [128, 2, SPX])
        fin = sb("fin", [128, 2, SPX])
        gate_in = sb("gate_in", [128, 2, TBLK * 2 * E])
        gateT = sq
        gx = vx[:, :, :, :].rearrange("p t n k -> p (t n k)")[:, 0:4 * SPX].rearrange("p (r n) -> p r n", r=4)
        ffn_out = fin

        banks = [ctx.enter_context(nc.psum_tensor(f"bank{n}", [128, 512], FP32)) for n in range(8)]
        bank_a, bank_s, bank_t, bank_o = banks[0:2], banks[2:4], banks[4:6], banks[6:8]
        gate_bank = banks[0:4]

        bias_loaded = sem("bias_loaded")
        const_loaded, const_made, const_step = sem("const_loaded"), sem("const_made"), sem("const_step")
        weights_cleared = sem("weights_cleared")
        xs_loaded, xs_read = sem("xs_loaded"), sem("xs_read")
        xc_made, sq_made, var_made = sem("xc_made"), sem("sq_made"), sem("var_made")
        ln_made, rstd_made, xn_made = sem("ln_made"), sem("rstd_made"), sem("xn_made")
        v_made, v_saved = sem("v_made"), sem("v_saved")
        q_made, k_made = sem("q_made"), sem("k_made")
        q_saved, k_saved, v_copied = sem("q_saved"), sem("k_saved"), sem("v_copied")
        qx_made, kx_made, vx_made = sem("qx_made"), sem("kx_made"), sem("vx_made")
        score_made, max_made, shifted = sem("score_made"), sem("max_made"), sem("shifted")
        exp_made, sum_made, inv_made, prob_made = sem("exp_made"), sem("sum_made"), sem("inv_made"), sem("prob_made")
        probT_made, vT_made, vt_saved = sem("probT_made"), sem("vT_made"), sem("vt_saved")
        pv_made, picked, lepe_step, fin_made = sem("pv_made"), sem("picked"), sem("lepe_step"), sem("fin_made")
        z_stored = [sem("z_stored0"), sem("z_stored1")]
        f_x_loaded, f_loaded = sem("f_x_loaded"), sem("f_loaded")
        y_step, y_made = sem("y_step"), sem("y_made")
        fc_made, fsq_made, fvar_made = sem("fc_made"), sem("fsq_made"), sem("fvar_made")
        fln_made, frstd_made, yn_made = sem("fln_made"), sem("frstd_made"), sem("yn_made")
        logitT_made, logitT_saved, logit_made = sem("logitT_made"), sem("logitT_saved"), sem("logit_made")
        logit_saved, gap_made, gap_exp = sem("logit_saved"), sem("gap_made"), sem("gap_exp")
        gate_step, gates_made = sem("gate_step"), sem("gates_made")
        sum2_made, inv2_made = sem("sum2_made"), sem("inv2_made")
        gate_cut, gateT_made, gateT_saved = sem("gate_cut"), sem("gateT_made"), sem("gateT_saved")
        gate_spread, gx_made, ffn_made, y_out_made = sem("gate_spread"), sem("gx_made"), sem("ffn_made"), sem("y_out_made")
        out_stored = [sem("out_stored0"), sem("out_stored1")]

        passed = sem("passed")

        def wait_alone(eng, signal, count):
            eng.wait_ge(signal, count)
            eng.sem_inc(passed, 1)

        def windows(rows):
            return rows.rearrange("p (r n w) -> p n r w", r=SP, w=SP)

        def by_window(flat):
            return flat.rearrange("p (n r w) -> p n r w", r=SP, w=SP)

        vpad_rows = vpad[:, :].rearrange("p (r w) -> p r w", w=PADW)

        def vrows(t, dr, dw):
            return vpad[:, bass.ds((t * SP + dr + 1) * PADW, SP * PADW)].rearrange(
                "p (r w) -> p r w", w=PADW)[:, :, dw + 1:dw + 1 + W]

        def slots(eng, total, depth, period, body):
            head = -(-depth // period) * period
            loops = (total - head) // period
            for s in range(head):
                body(s, s, s)
            with eng.Fori(0, loops) as m:
                for s in range(period):
                    body(m * period + (head + s), s, None)
            for s in range(head + loops * period, total + depth):
                body(s, s, s)

        def on(ramp, d, total):
            return ramp is None or 0 <= ramp - d < total

        P1_DEPTH, P2_DEPTH, F_DEPTH = 2, 7, 3
        P2_PERIOD = 2 * UNITS
        P2_HEAD = -(-P2_DEPTH // P2_PERIOD) * P2_PERIOD
        loop_now = {}

        def slots_p2(eng, body):
            loops = (IMU - P2_HEAD) // P2_PERIOD
            for s in range(P2_HEAD):
                body(s, s, s)
            with eng.Fori(0, loops) as m:
                loop_now["m"] = m
                for s in range(P2_PERIOD):
                    body(m * P2_PERIOD + (P2_HEAD + s), s, None)
            for s in range(P2_HEAD + loops * P2_PERIOD, IMU + P2_DEPTH):
                body(s, s, s)

        def strip_of(par, d, ramp):
            if ramp is not None:
                return (ramp - d) // UNITS
            return loop_now["m"] * 2 + (P2_HEAD + par - d) // UNITS

        MM = nc.tensor.matmul

        block = ctx.enter_context(nc.Block())

        @block.sync
        def _(sp):
            sp.dma_start(const_sb[:, :], consts).then_inc(const_loaded, 16)
            with nc.allow_non_contiguous_dma("small weights, once"):
                tab = bias_table.rearrange("(a b) h -> a (b h)", a=2 * SP - 1)
                for rj in range(SP):
                    for wj in range(SP):
                        j = rj * SP + wj
                        sp.dma_start(bias_all[j:j + 1, :, :].rearrange("p (r w) h -> p r (w h)", r=SP),
                                     tab[SP - 1 - rj:2 * SP - 1 - rj, (SP - 1 - wj) * HEADS:(2 * SP - 1 - wj) * HEADS]
                                     .unsqueeze(0)).then_inc(bias_loaded, 16)
                sp.wait_ge(bias_loaded, 16 * TOK)
                for k in range(1, 8):
                    sp.dma_start(bias_all[k * TOK:(k + 1) * TOK, :, :], bias_all[0:TOK, :, :]).then_inc(const_loaded, 16)
                for g in range(4):
                    sp.dma_start(lepe_sb[g * CH:(g + 1) * CH, :],
                                 lepe_w.rearrange("c o r w -> c (o r w)")).then_inc(const_loaded, 16)
                for half in range(2):
                    sp.dma_start(router_bias[half * E:(half + 1) * E, :],
                                 router_b.rearrange("(e o) -> e o", o=1)).then_inc(const_loaded, 16)
                sp.wait_ge(weights_cleared, 1)
                for g in range(4):
                    for part in range(3):
                        sp.dma_start(wqkv[g * CH:(g + 1) * CH, part, g * CH:(g + 1) * CH],
                                     qkv_w[part * CH:(part + 1) * CH, :].rearrange("o i -> i o")).then_inc(const_loaded, 16)
                for half in range(2):
                    rows = slice(half * C, (half + 1) * C)
                    sp.dma_start(router_sb[rows, half * E:(half + 1) * E], router_w).then_inc(const_loaded, 16)
                    sp.dma_start(expert_sb[rows, :, rows], expert_w.rearrange("e d c -> d e c")).then_inc(const_loaded, 16)
                    sp.dma_start(expert_bias[half * E:(half + 1) * E, rows], expert_b).then_inc(const_loaded, 16)

            with sp.Fori(0, B) as b:
                for half in range(2):
                    sp.dma_start(y[half * C:(half + 1) * C, :],
                                 x[bass.ds(b, 1), :, half * HALFH:(half + 1) * HALFH, :]
                                 .rearrange("b c r w -> c (b r w)")).then_inc(f_x_loaded, 16)
                with sp.Fori(0, STRIPS // 2) as m:
                    for p in range(2):
                        wait_alone(sp, fin_made, b * STRIPS + m * 2 + (p + 1))
                        for roll in range(2):
                            sp.dma_start(z[roll, bass.ds(b, 1), :, bass.ds(m * (2 * SP) + p * SP, SP), :]
                                         .rearrange("b c r w -> c (b r w)"),
                                         fin[roll * C:(roll + 1) * C, p, :]).then_inc(z_stored[p], 16)
                for p in range(2):
                    wait_alone(sp, z_stored[p], (b + 1) * (STRIPS // 2 * 32))
                for half in range(2):
                    sp.dma_start(z0[half * C:(half + 1) * C, :],
                                 z[0, bass.ds(b, 1), :, half * HALFH:(half + 1) * HALFH, :]
                                 .rearrange("b c r w -> c (b r w)")).then_inc(f_loaded, 16)
                for c_to, c_from, nch in ((ROLL, 0, CH - ROLL), (0, CH - ROLL, ROLL),
                                          (CH + ROLL, CH, CH - ROLL), (CH, C - ROLL, ROLL)):
                    for half, r_to, r_from, nr in ((0, ROLL, 0, HALFH - ROLL), (0, 0, H - ROLL, ROLL),
                                                   (1, 0, HALFH - ROLL, HALFH)):
                        sp.dma_start(z2[half * C + c_to:half * C + c_to + nch, r_to * W:(r_to + nr) * W],
                                     z[1, bass.ds(b, 1), c_from:c_from + nch, r_from:r_from + nr, :]
                                     .rearrange("b c r w -> c (b r w)")).then_inc(f_loaded, 16)
                with sp.Fori(0, TILES // 2) as m:
                    for p in range(2):
                        wait_alone(sp, y_out_made, b * TILES + m * 2 + (p + 1))
                        for half in range(2):
                            sp.dma_start(out[bass.ds(b, 1), :, bass.ds(m * (2 * SP) + (p * SP + half * HALFH), SP), :]
                                         .rearrange("b c r w -> c (b r w)"),
                                         ffn_out[half * C:(half + 1) * C, p, :]).then_inc(out_stored[p], 16)
                for p in range(2):
                    wait_alone(sp, out_stored[p], (b + 1) * (TILES // 2 * 32))

        N_CONST_DMAS = 1 + 7 + 4 + 2 + 12 + 6

        @block.gpsimd
        def _(pool):
            G = nc.gpsimd
            for buf in (wqkv, router_sb, expert_sb):
                G.memset(buf[:].rearrange("p a b -> p (a b)") if len(buf.shape) == 3 else buf[:, :], 0.0)\
                    .then_inc(const_step, 1)
            G.memset(expert_bias[:, :], 0.0).then_inc(const_step, 1)
            pool.wait_ge(const_step, 4)
            pool.sem_inc(weights_cleared, 1)

            def load_image(b):
                pool.dma_start(xs[0:C, :], x[bass.ds(b, 1), :, :, :].rearrange("b c r w -> c (b r w)"))\
                    .then_inc(xs_loaded, 16)
                for c_to, c_from, nch in ((0, ROLL, C - ROLL), (C - ROLL, 0, ROLL)):
                    for r_to, r_from, nr in ((0, ROLL, H - ROLL), (H - ROLL, 0, ROLL)):
                        pool.dma_start(xs[C + c_to:C + c_to + nch, r_to * W:(r_to + nr) * W],
                                       x[bass.ds(b, 1), c_from:c_from + nch, r_from:r_from + nr, :]
                                       .rearrange("b c r w -> c (b r w)")).then_inc(xs_loaded, 16)

            def spread(dst, src, mask, groups, unit):
                shape = [128, UW, groups, TOK]
                return G.tensor_tensor(
                    dst, src[:, unit * UPX:(unit + 1) * UPX].rearrange("p (n i) -> p n i", i=TOK)
                    .unsqueeze(2).broadcast_to(shape),
                    mask.unsqueeze(1).unsqueeze(3).broadcast_to(shape), ALU.mult)

            def image(b):
                def slot(s, par, ramp):
                    def u(d):
                        return (b * IMU + (s - d)), (par - d) % 2, (par - d) % 3, ((par - d) // 3) % 2

                    if on(ramp, 4, IMU):
                        n, h, j, strip = u(4)
                        pool.wait_ge(inv_made, n + 1)
                        pv = prob[:, h, :].rearrange("p (r j) -> p r j", j=TOK)
                        G.tensor_tensor(pv, pv, row_inv[:, h, :].unsqueeze(2).broadcast_to([128, UW * 4, TOK]),
                                        ALU.mult).then_inc(prob_made, 1)
                        if ramp is None or ramp - 4 >= 2:
                            pool.wait_ge(vT_made, (n - 1) * 2)
                        pool.wait_ge(v_copied, b * STRIPS + strip_of(par, 4, ramp) + 1)
                        spread(vx[:, h, :, :].rearrange("p n (k i) -> p n k i", i=TOK), v_sb[:, strip, :],
                               const("mask_v"), 8, j).then_inc(vx_made, 1)
                    if on(ramp, 2, IMU):
                        n, h, j, strip = u(2)
                        pool.wait_ge(q_saved, b * STRIPS + strip_of(par, 2, ramp) + 1)
                        spread(qx[:, h, :, :].rearrange("p n (k i) -> p n k i", i=TOK), q_sb[:, strip, :],
                               const("mask_q"), 8, j).then_inc(qx_made, 1)

                slots_p2(pool, slot)

            pool.wait_ge(const_loaded, 16 * N_CONST_DMAS)
            load_image(0)
            with pool.Fori(0, B - 1) as b:
                image(b)
                pool.wait_ge(xs_read, b + 1)
                load_image(b + 1)
            image(B - 1)

        @block.tensor
        def _(pe):
            pe.wait_ge(const_loaded, 16 * N_CONST_DMAS)
            pe.wait_ge(const_made, 3)
            with pe.Fori(0, B) as b:
                pe.wait_ge(xs_loaded, (b + 1) * 80)

                def slot(s, par, ramp):
                    if on(ramp, 2, STRIPS):
                        n, h = b * STRIPS + (s - 2), par % 2
                        pe.wait_ge(xn_made, n + 1)
                        MM(bank_o[h][:, 0:SPX], wqkv[:, 2, :], xs[:, bass.ds((s - 2) * SPX, SPX)],
                           start=True, stop=True).then_inc(v_made, 1)
                    if on(ramp, 1, STRIPS):
                        n, h = b * STRIPS + (s - 1), (par - 1) % 2
                        pe.wait_ge(sq_made, n + 1)
                        MM(bank_s[h][:, 0:SPX], const("mean"), sq[:, h, :], start=True, stop=True).then_inc(var_made, 1)
                    if on(ramp, 0, STRIPS):
                        h = par % 2
                        MM(bank_a[h][:, 0:SPX], const("center"), xs[:, bass.ds(s * SPX, SPX)],
                           start=True, stop=True).then_inc(xc_made, 1)

                slots(pe, STRIPS, P1_DEPTH, 2, slot)
                pe.wait_ge(v_saved, (b + 1) * STRIPS)

                def slot(s, par, ramp):
                    if on(ramp, 6, IMU):
                        n, h = b * IMU + (s - 6), par % 2
                        pe.wait_ge(probT_made, n + 1)
                        pe.wait_ge(vt_saved, (n + 1) * 2)
                        for w in range(UW):
                            last = MM(bank_o[h][:, w * KEYS:(w + 1) * KEYS], vt[:, h, w, :], probT[:, h, w, :],
                                      start=True, stop=True)
                        last.then_inc(pv_made, 1)
                    if on(ramp, 3, IMU):
                        n, h = b * IMU + (s - 3), (par - 3) % 2
                        pe.wait_ge(qx_made, n + 1)
                        pe.wait_ge(kx_made, n + 1)
                        MM(bank_s[h][:, :], bias_hi_mid[:, :], key_sel[:, :], start=True, stop=False)
                        MM(bank_s[h][:, :], bias_lo[:, :], key_sel[0:64, :], start=False, stop=False)
                        for w in range(UW):
                            last = MM(bank_s[h][:, w * KEYS:(w + 1) * KEYS], qx[:, h, w, :], kx[:, h, w, :],
                                      start=False, stop=(w == UW - 1))
                        last.then_inc(score_made, 1)
                    if par % UNITS == 0 and on(ramp, 0, IMU):
                        if ramp is None:
                            at = loop_now["m"] * (2 * SPX) + ((P2_HEAD + par) // UNITS) * SPX
                        else:
                            at = ramp // UNITS * SPX
                        MM(bank_a[0][:, 0:SPX], wqkv[:, 0, :], xs[:, bass.ds(at, SPX)],
                           start=True, stop=True).then_inc(q_made, 1)
                        MM(bank_a[1][:, 0:SPX], wqkv[:, 1, :], xs[:, bass.ds(at, SPX)],
                           start=True, stop=True).then_inc(k_made, 1)
                    if on(ramp, 5, IMU):
                        n, h = b * IMU + (s - 5), (par - 5) % 2
                        pe.wait_ge(vx_made, n + 1)
                        for t in range(2):
                            for w in range(4):
                                last = nc.tensor.transpose(bank_t[t][:, w * 128:(w + 1) * 128],
                                                           vx[:, h, 4 * t + w, :], const("ident"))
                            last.then_inc(vT_made, 1)

                slots_p2(pe, slot)
                pe.wait_ge(k_made, (b + 1) * STRIPS)
                pe.sem_inc(xs_read, 1)
                pe.wait_ge(fin_made, (b + 1) * STRIPS)

                def slot(s, par, ramp):
                    if on(ramp, 3, TILES):
                        n, h = b * TILES + (s - 3), (par - 3) % 2
                        wait_alone(pe, logitT_saved, n + 1)
                        for k in range(TBLK):
                            last = nc.tensor.transpose(bank_o[h][:, k * 2 * E:(k + 1) * 2 * E],
                                                       logitT[0:2 * E, h, k * 128:(k + 1) * 128],
                                                       const("ident", 2 * E)[:, 0:2 * E])
                        last.then_inc(logit_made, 1)
                    if on(ramp, 2, TILES):
                        n, h = b * TILES + (s - 2), par % 2
                        pe.wait_ge(yn_made, n + 1)
                        MM(bank_t[h][0:2 * E, 0:SPX], router_sb[:, :], yn[:, bass.ds((s - 2) * SPX, SPX)],
                           start=True, stop=True).then_inc(logitT_made, 1)
                    if on(ramp, 1, TILES):
                        n, h = b * TILES + (s - 1), (par - 1) % 2
                        pe.wait_ge(fsq_made, n + 1)
                        MM(bank_s[h][:, 0:SPX], const("mean"), sq[:, h, :], start=True, stop=True).then_inc(fvar_made, 1)
                    if on(ramp, 0, TILES):
                        pe.wait_ge(y_made, b * TILES + s + 1)
                        MM(bank_a[par % 2][:, 0:SPX], const("center"), y[:, bass.ds(s * SPX, SPX)],
                           start=True, stop=True).then_inc(fc_made, 1)

                slots(pe, TILES, F_DEPTH, 2, slot)

                def turn_gates(n, h):
                    pe.wait_ge(gate_cut, n + 1)
                    for k in range(TBLK):
                        last = nc.tensor.transpose(bank_t[h][0:2 * E, k * 128:(k + 1) * 128],
                                                   gate_in[:, h, k * 2 * E:(k + 1) * 2 * E], const("ident"))
                    last.then_inc(gateT_made, 1)

                def tile(j, h, more):
                    n = b * TILES + j
                    pe.wait_ge(gateT_saved, n + 1)
                    MM(bank_o[h][:, 0:SPX], expert_bias[:, :], gateT[0:2 * E, h, :], start=True, stop=False)

                    def spread_gate(e):
                        at, _ = CONST_AT["expert_sel"]
                        MM(gate_bank[e % 4][:, 0:SPX], const_sb[0:2 * E, at + e * 128:at + (e + 1) * 128],
                           gateT[0:2 * E, h, :], start=True, stop=True).then_inc(gate_spread, 1)

                    for e in range(3):
                        spread_gate(e)
                    for e in range(E):
                        pe.wait_ge(gx_made, n * E + (e + 1))
                        last = MM(bank_o[h][:, 0:SPX], expert_sb[:, e, :], gx[:, e % 4, :],
                                  start=False, stop=(e == E - 1))
                        if e + 3 < E:
                            spread_gate(e + 3)
                        if e == 3 and more:
                            turn_gates(n + 1, 1 - h)
                    last.then_inc(ffn_made, 1)

                turn_gates(b * TILES, 0)
                with pe.Fori(0, TILES // 2 - 1) as m:
                    for p in range(2):
                        tile(m * 2 + p, p, True)
                tile(TILES - 2, 0, True)
                tile(TILES - 1, 1, False)
                pe.wait_ge(y_out_made, (b + 1) * TILES)

        @block.scalar
        def _(act):
            S = nc.scalar
            S.preload_act_table_set("natural_log_exp_and_others")
            act.wait_ge(const_loaded, 16 * N_CONST_DMAS)
            S.activation(key_sel[:, :].rearrange("p (n k) -> p n k", k=KEYS),
                         const("ident64x2").unsqueeze(1).broadcast_to([128, UW, KEYS]), ACT.Copy).then_inc(const_made, 1)

            def norm_slot(total, last_lag, lag_body, eps, made, sqm, varm, lnm, rsm, n_of):
                def slot(s, par, ramp):
                    lag_body(s, par, ramp)
                    if on(ramp, 0, total):
                        h = par % 2
                        act.wait_ge(made, n_of(s) + 1)
                        S.activation(sq[:, h, :], bank_a[h][:, 0:SPX], ACT.Square).then_inc(sqm, 1)
                    if on(ramp, 1, total):
                        n, h = n_of(s - 1), (par - 1) % 2
                        act.wait_ge(varm, n + 1)
                        S.activation(rstd[:, h, :], bank_s[h][:, 0:SPX], ACT.Ln, bias=eps).then_inc(lnm, 1)
                        act.wait_ge(lnm, n + 1)
                        S.activation(rstd[:, h, :], rstd[:, h, :], ACT.Exp, scale=-0.5).then_inc(rsm, 1)
                return slot

            with act.Fori(0, B) as b:
                def save_v(s, par, ramp):
                    if on(ramp, 2, STRIPS):
                        act.wait_ge(v_made, b * STRIPS + (s - 2) + 1)
                        S.activation(vrows(s - 2, 0, 0), bank_o[par % 2][:, 0:SPX].rearrange("p (r w) -> p r w", w=W),
                                     ACT.Copy).then_inc(v_saved, 1)

                slots(act, STRIPS, P1_DEPTH, 2,
                      norm_slot(STRIPS, 2, save_v, const("eps1"), xc_made, sq_made, var_made, ln_made, rstd_made,
                                lambda s: b * STRIPS + s))
                act.wait_ge(v_saved, (b + 1) * STRIPS)

                def slot(s, par, ramp):
                    strip = (par // UNITS) % 2
                    if par % UNITS == 0 and on(ramp, 0, IMU):
                        n = b * STRIPS + strip_of(par, 0, ramp)
                        act.wait_ge(q_made, n + 1)
                        S.activation(by_window(q_sb[:, strip, :]), windows(bank_a[0][:, 0:SPX]), ACT.Copy,
                                     scale=float(HD) ** -0.5).then_inc(q_saved, 1)
                        act.wait_ge(k_made, n + 1)
                        S.activation(by_window(k_sb[:, strip, :]), windows(bank_a[1][:, 0:SPX]), ACT.Copy)\
                            .then_inc(k_saved, 1)
                    if on(ramp, 3, IMU):
                        n, h = b * IMU + (s - 3), (par - 3) % 2
                        act.wait_ge(shifted, n + 1)
                        S.activation(prob[:, h, :], prob[:, h, :], ACT.Exp).then_inc(exp_made, 1)
                    if on(ramp, 5, IMU):
                        n, h = b * IMU + (s - 5), (par - 5) % 2
                        for t in range(2):
                            act.wait_ge(vT_made, n * 2 + (t + 1))
                            S.activation(vt[:, h, 4 * t:4 * t + 4, :].rearrange("p n k -> p (n k)"), bank_t[t][:, :],
                                         ACT.Copy).then_inc(vt_saved, 1)
                    if par % UNITS == 0 and on(ramp, 3, IMU):
                        t = strip_of(par, 3, ramp)
                        v_strip = ((par - 3) // UNITS) % 2
                        S.activation(by_window(v_sb[:, v_strip, :]),
                                     vrows(t, 0, 0).rearrange("p r (n w) -> p n r w", w=SP), ACT.Copy)\
                            .then_inc(v_copied, 1)

                slots_p2(act, slot)

                def save_logits(s, par, ramp):
                    if on(ramp, 2, TILES):
                        h = par % 2
                        act.wait_ge(logitT_made, b * TILES + (s - 2) + 1)
                        S.activation(logitT[0:2 * E, h, :], bank_t[h][0:2 * E, 0:SPX], ACT.Identity,
                                     bias=router_bias[:, :]).then_inc(logitT_saved, 1)

                slots(act, TILES, F_DEPTH, 2,
                      norm_slot(TILES, 2, save_logits, const("eps2"), fc_made, fsq_made, fvar_made, fln_made,
                                frstd_made, lambda s: b * TILES + s))

                act.wait_ge(gap_made, b + 1)
                S.activation(gate_vec(2), gate_vec(2), ACT.Exp).then_inc(gap_exp, 1)
                act.wait_ge(gates_made, b + 1)

                def cut(j, h):
                    S.activation(gate_in[:, h, :], gate_buf(6)[:, bass.ds(j * (TBLK * 2 * E), TBLK * 2 * E)], ACT.Copy)\
                        .then_inc(gate_cut, 1)
                    act.wait_ge(gateT_made, b * TILES + j + 1)
                    S.activation(gateT[0:2 * E, h, :], bank_t[h][0:2 * E, 0:SPX], ACT.Copy).then_inc(gateT_saved, 1)

                with act.Fori(0, TILES // 2) as m:
                    for p in range(2):
                        cut(m * 2 + p, p)

        @block.vector
        def _(dve):
            V = nc.vector
            V.memset(vpad[:, :], 0.0).then_inc(const_made, 1)
            dve.wait_ge(const_loaded, 16 * N_CONST_DMAS)
            step = [4]

            def chained(ins):
                step[0] += 1
                ins.then_inc(const_step, 1)
                dve.wait_ge(const_step, step[0])

            by_head = bias_all[:, :, :].rearrange("p i (A m) -> p (i A) m", A=2)
            chained(V.tensor_tensor(by_head, by_head, const("mask_b").unsqueeze(1).broadcast_to([128, 2 * TOK, 4]),
                                    ALU.mult))
            chained(V.tensor_reduce(bias_sb[:, :].rearrange("p (A i) -> p i A", A=2),
                                    bias_all[:, :, :].rearrange("p i (A m) -> p i A m", A=2), AX.X, ALU.add))
            rest = bias_sb[:, :]
            for k in range(3):
                chained(V.tensor_copy(bias_part[:, k, :], rest))
                if k < 2:
                    chained(V.tensor_tensor(bias_rest[:, k, :], rest, bias_part[:, k, :], ALU.subtract))
                    rest = bias_rest[:, k, :]
            for dst, rows, k in ((bias_hi_mid, slice(0, 64), 0), (bias_hi_mid, slice(64, 128), 1),
                                 (bias_lo, slice(0, 64), 2)):
                last = V.tensor_copy(dst[rows, :].rearrange("p (g a) -> p g a", g=4),
                                     bias_part[rows, k, :].unsqueeze(1).broadcast_to([64, 4, 2 * TOK]))
            last.then_inc(const_made, 1)

            with dve.Fori(0, B) as b:
                def slot(s, par, ramp):
                    if on(ramp, 1, STRIPS):
                        h = (par - 1) % 2
                        dve.wait_ge(rstd_made, b * STRIPS + (s - 1) + 1)
                        V.tensor_tensor(xs[:, bass.ds((s - 1) * SPX, SPX)], bank_a[h][:, 0:SPX], rstd[:, h, :],
                                        ALU.mult).then_inc(xn_made, 1)

                slots(dve, STRIPS, P1_DEPTH, 2, slot)

                def slot(s, par, ramp):
                    if on(ramp, 7, IMU):
                        n, h, j, strip = b * IMU + (s - 7), (par - 7) % 2, (par - 7) % 3, ((par - 7) // 3) % 2
                        dve.wait_ge(pv_made, n + 1)
                        pv = bank_o[h][:, :].rearrange("p (n m i) -> p m n i", m=4, i=TOK)
                        acc = att[:, strip, j * UPX:(j + 1) * UPX].rearrange("p (n i) -> p n i", i=TOK)
                        mask = const("mask_o")
                        for m in range(4):
                            if m == 0:
                                last = V.tensor_scalar(acc, pv[:, m], mask[:, 0:1], None, ALU.mult)
                            else:
                                dve.wait_ge(picked, n * 4 + m)
                                last = V.scalar_tensor_tensor(acc, pv[:, m], mask[:, m:m + 1], acc, ALU.mult, ALU.add)
                            last.then_inc(picked, 1)
                    if on(ramp, 5, IMU):
                        n, h = b * IMU + (s - 5), (par - 5) % 2
                        dve.wait_ge(prob_made, n + 1)
                        V.transpose(probT[:, h, :, :].rearrange("p n k -> p (n k)"), prob[:, h, :]).then_inc(probT_made, 1)
                    if on(ramp, 4, IMU):
                        n, h = b * IMU + (s - 4), (par - 4) % 2
                        dve.wait_ge(exp_made, n + 1)
                        V.tensor_reduce(row_sum[:, h, :], prob[:, h, :].rearrange("p (r j) -> p r j", j=TOK),
                                        AX.X, ALU.add).then_inc(sum_made, 1)
                    if on(ramp, 2, IMU):
                        n, h, j, strip = b * IMU + (s - 2), (par - 2) % 2, (par - 2) % 3, ((par - 2) // 3) % 2
                        dve.wait_ge(k_saved, b * STRIPS + strip_of(par, 2, ramp) + 1)
                        shape = [128, UW, 4, TOK]
                        V.tensor_tensor(kx[:, h, :, :].rearrange("p n (k i) -> p n k i", i=TOK),
                                        k_sb[:, strip, j * UPX:(j + 1) * UPX].rearrange("p (n i) -> p n i", i=TOK)
                                        .unsqueeze(2).broadcast_to(shape),
                                        const("mask_k").unsqueeze(1).unsqueeze(3).broadcast_to(shape),
                                        ALU.mult).then_inc(kx_made, 1)
                    if on(ramp, 4, IMU):
                        n, h = b * IMU + (s - 4), (par - 4) % 2
                        dve.wait_ge(sum_made, n + 1)
                        V.reciprocal(row_inv[:, h, :], row_sum[:, h, :]).then_inc(inv_made, 1)
                    if on(ramp, 3, IMU):
                        n, h = b * IMU + (s - 3), (par - 3) % 2
                        dve.wait_ge(score_made, n + 1)
                        sv = bank_s[h][:, :].rearrange("p (r j) -> p r j", j=TOK)
                        V.tensor_reduce(row_max[:, h, :], sv, AX.X, ALU.max).then_inc(max_made, 1)
                        dve.wait_ge(max_made, n + 1)
                        V.tensor_tensor(prob[:, h, :].rearrange("p (r j) -> p r j", j=TOK), sv,
                                        row_max[:, h, :].unsqueeze(2).broadcast_to([128, UW * 4, TOK]),
                                        ALU.subtract).then_inc(shifted, 1)
                    if on(ramp, 7, IMU):
                        j, strip = (par - 7) % 3, ((par - 7) // 3) % 2
                        t = strip_of(par, 7, ramp)
                        acc = lepe[:, strip, :].rearrange("p (r w) -> p r w", w=W)
                        for k in range(3):
                            tap = 3 * j + k
                            src = vrows(t, j - 1, k - 1)
                            wt = lepe_sb[:, tap:tap + 1]
                            if tap == 0:
                                last = V.tensor_scalar(acc, src, wt, None, ALU.mult)
                            else:
                                dve.wait_ge(lepe_step, (b * STRIPS + t) * 9 + tap)
                                last = V.scalar_tensor_tensor(acc, src, wt, acc, ALU.mult, ALU.add)
                            last.then_inc(lepe_step, 1)
                        if j == UNITS - 1:
                            if ramp is None or ramp - 7 >= 2 * UNITS:
                                dve.wait_ge(z_stored[strip], b * (STRIPS // 2 * 32) + (t - strip) * 16)
                            elif ramp - 7 < UNITS:
                                dve.wait_ge(f_x_loaded, (b + 1) * 32)
                            dve.wait_ge(lepe_step, (b * STRIPS + t) * 9 + 9)
                            dve.wait_ge(picked, (b * STRIPS + t) * (4 * UNITS) + 4 * UNITS)
                            V.tensor_tensor(windows(fin[:, strip, :]), by_window(att[:, strip, :]),
                                            windows(lepe[:, strip, :]), ALU.add).then_inc(fin_made, 1)

                slots_p2(dve, slot)

                dve.wait_ge(f_x_loaded, (b + 1) * 32)
                wait_alone(dve, f_loaded, (b + 1) * (14 * 16))

                def slot(s, par, ramp):
                    if on(ramp, 3, TILES):
                        n, h = b * TILES + (s - 3), (par - 3) % 2
                        dve.wait_ge(logit_made, n + 1)
                        V.tensor_copy(logits_of(s - 3), bank_o[h][:, 0:TBLK * 2 * E]).then_inc(logit_saved, 1)
                    if on(ramp, 0, TILES):
                        n = b * TILES + s
                        here = bass.ds(s * SPX, SPX)
                        V.tensor_tensor(y[:, here], y[:, here], z0[:, here], ALU.add).then_inc(y_step, 1)
                        dve.wait_ge(y_step, n + 1)
                        V.tensor_tensor(y[:, here], y[:, here], z2[:, here], ALU.add).then_inc(y_made, 1)
                    if on(ramp, 1, TILES):
                        h = (par - 1) % 2
                        dve.wait_ge(frstd_made, b * TILES + (s - 1) + 1)
                        V.tensor_tensor(yn[:, bass.ds((s - 1) * SPX, SPX)], bank_a[h][:, 0:SPX], rstd[:, h, :],
                                        ALU.mult).then_inc(yn_made, 1)

                def logits_of(j):
                    return logits[:, bass.ds(j * (TBLK * 2 * E), TBLK * 2 * E)]

                slots(dve, TILES, F_DEPTH, 2, slot)
                dve.wait_ge(logit_saved, (b + 1) * TILES)

                GS = 13
                done = [0]

                def step(ins):
                    done[0] += 1
                    ins.then_inc(gate_step, 1)
                    dve.wait_ge(gate_step, b * GS + done[0])

                def per_e(v):
                    return v.rearrange("p (t e) -> p t e", e=E)

                def wide(vec):
                    return vec.unsqueeze(2).broadcast_to([128, GATES, E])

                rank = const("rank").unsqueeze(1).broadcast_to([128, GATES, E])
                lg = logits[:, :]
                one1, one2, tmp, rest2, gates = (gate_buf(k) for k in (1, 2, 3, 4, 6))
                best1, best2, gap, vec = (gate_vec(k) for k in range(4))
                for best, src, hot in ((best1, lg, one1), (best2, rest2, one2)):
                    step(V.tensor_reduce(best, per_e(src), AX.X, ALU.max))
                    step(V.tensor_tensor(per_e(tmp), per_e(src), wide(best), ALU.is_equal))
                    step(V.tensor_tensor(per_e(tmp), per_e(tmp), rank, ALU.mult))
                    step(V.tensor_reduce(vec, per_e(tmp), AX.X, ALU.max))
                    step(V.tensor_tensor(per_e(hot), per_e(tmp), wide(vec), ALU.is_equal))
                    if best is best1:
                        step(V.scalar_tensor_tensor(rest2, one1, -3.0e38, lg, ALU.mult, ALU.add))
                assert done[0] == 11
                V.tensor_tensor(gap, best2, best1, ALU.subtract).then_inc(gap_made, 1)
                dve.wait_ge(gap_exp, b + 1)
                step(V.scalar_tensor_tensor(per_e(gates), per_e(one2), 1.0, wide(gap), ALU.mult, ALU.mult))
                V.tensor_scalar(vec, gap, 1.0, None, ALU.add).then_inc(sum2_made, 1)
                dve.wait_ge(sum2_made, b + 1)
                V.reciprocal(best1, vec).then_inc(inv2_made, 1)
                step(V.tensor_tensor(gates, gates, one1, ALU.add))
                dve.wait_ge(inv2_made, b + 1)
                V.tensor_tensor(per_e(gates), per_e(gates), wide(best1), ALU.mult).then_inc(gates_made, 1)
                assert done[0] == GS

                def tile(j, h, wait_store):
                    n = b * TILES + j
                    here = bass.ds(j * SPX, SPX)
                    for e in range(E):
                        dve.wait_ge(gate_spread, n * E + (e + 1))
                        V.tensor_tensor(gx[:, e % 4, :], gate_bank[e % 4][:, 0:SPX], yn[:, here], ALU.mult)\
                            .then_inc(gx_made, 1)
                    dve.wait_ge(ffn_made, n + 1)
                    if wait_store is not None:
                        dve.wait_ge(out_stored[h], b * (TILES // 2 * 32) + wait_store)
                    V.tensor_tensor(ffn_out[:, h, :], bank_o[h][:, 0:SPX], y[:, here], ALU.add).then_inc(y_out_made, 1)

                tile(0, 0, None)
                tile(1, 1, None)
                with dve.Fori(1, TILES // 2) as m:
                    for p in range(2):
                        tile(m * 2 + p, p, m * 32)



_INS = ["x", "L0_conv_qkv_w", "L0_conv_lepe_w", "L0_conv_bias_table", "L0_ffn_router_w", "L0_ffn_router_b",
        "L0_ffn_expert_w", "L0_ffn_expert_b"]


def kernel(**inputs):
    import numpy as _np
    import concourse.bacc as _bacc
    from concourse import mybir as _mybir
    from concourse.bass_utils import run_bass_kernel_spmd as _run

    nc = _bacc.Bacc("TRN2", target_bir_lowering=False, num_devices=1)
    arrays, args = {}, []
    for name in _INS:
        arrays[f"in_{name}"] = _np.ascontiguousarray(inputs[name])
    arrays["in_constants"] = CONSTS
    for name, a in arrays.items():
        args.append(nc.dram_tensor(name, a.shape, _mybir.dt.from_np(a.dtype), kind="ExternalInput").ap())
    args.append(nc.dram_tensor("out_y", (B, C, H, W), _mybir.dt.float32, kind="ExternalOutput").ap())
    metaformer_block(nc, *args)
    r = _run(nc, [arrays], core_ids=[0])
    return r.results[0]["out_y"]
```

```python
from contextlib import ExitStack

import numpy as np
import concourse.bass as bass
from concourse import mybir

FP32 = mybir.dt.float32
BF16 = mybir.dt.bfloat16
ALU = mybir.AluOpType
ACT = mybir.ActivationFunctionType
AX = mybir.AxisListType

B, C, H, W = 8, 64, 96, 96
CH = C // 2
HEADS, HD = 8, 4
SP = 4
TOK = SP * SP
E = 8
ROLL = 2
STRIPS = H // SP
SPX = SP * W
WIN = W // SP
UW = 8
UNITS = WIN // UW
UPX = UW * TOK
KEYS = 4 * TOK
UK = UW * KEYS
PADW = W + 2
TSLOT = 2 * UNITS
TBLK = SPX // 128
GE = 2 * E
N_UNIT, N_STRIP, N_TILE = B * STRIPS * UNITS, B * STRIPS, B * STRIPS // 2
IMT = STRIPS // 2
LN1_EPS, LN2_EPS = 1e-6, 1e-5
POOL_TAPS = 3

LAG = dict(
    centre=0, variance=1, value=2, query_key=3,
    mask_q=5, score=6, total=7, mask_v=7, turn_p=8, turn_v=8, product=9, pick=10,
    pool_taps=7, copy_v=6, taps=10, add_taps=12,
    store_z=12, load_tile=22, tile_sum=24, tile_variance=25, router=26, logits=27, gates=28,
    turn_gates=29, save_gates=30, experts=31, tile_out=35)
PERIOD = 2 * TSLOT
DEPTH = LAG["tile_out"]
HEAD = (-(-DEPTH // PERIOD) + 1) * PERIOD
EXPERT_AT = {(0, 0): 0, (0, 1): 1, (1, 0): 2, (2, 0): 3, (2, 1): 4, (3, 0): 5, (3, 1): 6, (4, 0): 7}


class Slot:

    def __init__(self, number, turn=None):
        self.n, self.turn = number, turn

    def _item(self, lag, span, total):
        at = self.n - LAG[lag]
        if self.turn is None and not 0 <= at // span < total:
            return None
        k = at // span
        return (k if self.turn is None else self.turn * (PERIOD // span) + k), k

    def unit(self, lag):
        return self._item(lag, 1, N_UNIT)

    def strip(self, lag):
        return self._item(lag, UNITS, N_STRIP) if (self.n - LAG[lag]) % UNITS == 0 else None

    def in_strip(self, lag):
        got = self._item(lag, UNITS, N_STRIP)
        return got and (*got, (self.n - LAG[lag]) % UNITS)

    def tile(self, lag):
        return self._item(lag, TSLOT, N_TILE) if (self.n - LAG[lag]) % TSLOT == 0 else None

    def in_tile(self, lag):
        got = self._item(lag, TSLOT, N_TILE)
        return got and (*got, (self.n - LAG[lag]) % TSLOT)

    def later(self, residue, least):
        assert self.turn is None or residue >= least
        return residue >= least


def strips_to(s, count):
    return min(count, N_STRIP) if s.turn is None else count


def pipeline(eng, body):
    turns = (N_UNIT - HEAD) // PERIOD - 1
    for n in range(HEAD):
        body(Slot(n))
    with eng.Fori(0, turns) as turn:
        for n in range(HEAD, HEAD + PERIOD):
            body(Slot(n, turn))
    for n in range(HEAD + turns * PERIOD, N_UNIT + DEPTH + 1):
        body(Slot(n))




def _constants():
    p = np.arange(128)
    g, c = p // CH, p % CH
    head = c % HEADS
    vg, vx, vbeta = p // 16 % 4, p // 2 % 8, p % 2
    same64 = (p[:, None] // C == p[None, :] // C).astype(np.float32)
    parts = {
        "ident": np.eye(128),
        "centre": np.eye(128) - same64 / C,
        "mean": same64 / C,
        "mask_q": (g[:, None] == p[None, :8] // 2) & ((head >> 2)[:, None] == p[None, :8] % 2),
        "mask_k": (head & 3)[:, None] == p[None, :4],
        "mask_v": (vg[:, None] == p[None, :8] // 2) & (vbeta[:, None] == p[None, :8] % 2),
        "mask_o": (vx & 1)[:, None] == p[None, :2],
        "ident64x2": np.concatenate([np.eye(64), np.eye(64)]),
        "mask_b": (p[:, None] // TOK % 4) == p[None, :4],
        "expert_sel": np.stack([(p[:, None] % E == e) & (p[:, None] // E % 2 == p[None, :] // C)
                                & (p[:, None] < 3 * GE) for e in range(E)], axis=1).reshape(128, E * 128),
        "rank": np.tile(E - np.arange(E), (128, 1)),
        "eps1": np.full((128, 1), LN1_EPS),
        "eps2": np.full((128, 1), LN2_EPS),
    }
    at, cols = {}, 0
    for name, a in parts.items():
        at[name] = (cols, a.shape[1])
        cols += a.shape[1]
    return at, np.concatenate([a.astype(np.float32) for a in parts.values()], axis=1)


CONST_AT, CONSTS = _constants()


def metaformer_block(nc, x, qkv_w, lepe_w, bias_table, router_w, router_b, expert_w, expert_b, consts, out):
    ctx = ExitStack()
    with ctx:
        def sb(name, shape, dt=FP32):
            return ctx.enter_context(nc.sbuf_tensor(name, shape, dt))

        def sem(name):
            return ctx.enter_context(nc.semaphore(name))

        def sems(name):
            return [sem(name + "0"), sem(name + "1")]

        z = nc.dram_tensor("z", [2, B, C, H, W], FP32, kind="Internal").ap()

        const_sb = sb("const_sb", [128, CONSTS.shape[1]])

        def const(name, rows=128):
            at, n = CONST_AT[name]
            return const_sb[0:rows, at:at + n]

        wqkv = sb("wqkv", [128, 3, 128])
        wv = sb("wv", [128, 128])
        lepe_sb = sb("lepe_sb", [128, 9])
        bias_all = sb("bias_all", [128, TOK, HEADS])
        bias_sb = sb("bias_sb", [128, 2 * TOK])
        bias_rest = sb("bias_rest", [128, 2, 2 * TOK])
        bias_part = sb("bias_part", [128, 3, 2 * TOK], BF16)
        bias_hi_mid = sb("bias_hi_mid", [128, 128], BF16)
        bias_lo = sb("bias_lo", [64, 128], BF16)
        key_sel = sb("key_sel", [128, UK], BF16)
        router_sb = sb("router_sb", [128, GE])
        router_bias = sb("router_bias", [GE, 1])
        expert_sb = sb("expert_sb", [128, E, 128])
        expert_sel = sb("expert_sel", [3 * GE, E, 128], BF16)
        ebias_sb = sb("ebias_sb", [3 * GE, 128])
        ebias_rest = sb("ebias_rest", [3 * GE, 2, 128])
        ebias_part = sb("ebias_part", [3 * GE, 3, 128], BF16)
        ident_bf = sb("ident_bf", [128, 128], BF16)

        xs = sb("xs", [128, 4, SPX])
        vpad = sb("vpad", [128, (H + 2) * PADW])
        sq = sb("sq", [128, 2, SPX])
        rstd = sb("rstd", [128, 2, SPX])
        q_sb = sb("q_sb", [128, 2, SPX])
        v_sb = sb("v_sb", [128, 2, SPX])
        qx = sb("qx", [128, 2, UW, 128])
        kx = sb("kx", [128, 2, WIN, KEYS])
        vx = sb("vx", [128, 2, UW, 128])
        vt = sb("vt", [128, 2, UW, 128])
        prob = sb("prob", [128, 2, UK])
        probT = sb("probT", [128, 2, UW, KEYS])
        row_max = sb("row_max", [128, 2, UW * 4])
        row_sum = sb("row_sum", [128, 2, UW * 4])
        row_inv = sb("row_inv", [128, 2, UW * 4])
        att = sb("att", [128, 2, SPX])
        tap_sb = sb("tap_sb", [128, SPX])
        lepe_p = sb("lepe_p", [128, 2, SPX])
        lepe = sb("lepe", [128, 2, SPX])
        fin = sb("fin", [128, 2, SPX])
        xt = sb("xt", [128, 2, SPX])
        z0t = sb("z0t", [128, 2, SPX])
        z2t = sb("z2t", [128, 2, SPX])
        y = sb("y", [128, 2, SPX])
        yn = sb("yn", [128, 2, SPX])
        ysq = sb("ysq", [128, SPX])
        yrstd = sb("yrstd", [128, SPX])
        logitT = sb("logitT", [GE, SPX])
        logits = sb("logits", [128, TBLK * GE])
        gate_tmp = sb("gate_tmp", [128, 7, TBLK * GE])
        gate_vec = sb("gate_vec", [128, 6, TBLK * 2])
        gate_part = sb("gate_part", [128, TBLK, 3, GE], BF16)
        gateT = sb("gateT", [3 * GE, 2, SPX], BF16)
        gx = sb("gx", [128, 2, SPX])
        y_out = sb("y_out", [128, 2, SPX])

        banks = [ctx.enter_context(nc.psum_tensor(f"bank{n}", [128, 512], FP32)) for n in range(8)]
        bank_s, bank_o, bank_t, bank_p, bank_g, bank_f = banks[0:2], banks[2], banks[3], banks[4:6], banks[6], banks[7]

        bias_loaded, const_loaded, const_made, const_step = (
            sem("bias_loaded"), sem("const_loaded"), sem("const_made"), sem("const_step"))
        weights_cleared = sem("weights_cleared")
        x_loaded = sems("x_loaded")
        xc_made, xc_saved, sq_made, var_made = sem("xc_made"), sem("xc_saved"), sem("sq_made"), sem("var_made")
        ln_made, rstd_made, xn_made = sem("ln_made"), sem("rstd_made"), sem("xn_made")
        v_made, v_saved, q_made, k_made = sem("v_made"), sem("v_saved"), sem("q_made"), sem("k_made")
        q_saved, kx_made, v_copied = sem("q_saved"), sem("kx_made"), sem("v_copied")
        qx_made, vx_made = sem("qx_made"), sem("vx_made")
        score_made, max_made, shifted = sem("score_made"), sem("max_made"), sem("shifted")
        exp_made, sum_made, inv_made, prob_made = sem("exp_made"), sem("sum_made"), sem("inv_made"), sem("prob_made")
        probT_made, vT_made, vt_saved = sem("probT_made"), sem("vT_made"), sem("vt_saved")
        pv_made, picked = sem("pv_made"), sem("picked")
        pool_tap, pool_lepe_made, lepe_step, fin_step, fin_made = (
            sem("pool_tap"), sem("pool_lepe_made"), sem("lepe_step"), sem("fin_step"), sem("fin_made"))
        z_stored, tile_loaded, out_stored = sems("z_stored"), sems("tile_loaded"), sems("out_stored")
        y_step, y_made = sem("y_step"), sem("y_made")
        fc_made, fc_saved, fsq_made, fvar_made = sem("fc_made"), sem("fc_saved"), sem("fsq_made"), sem("fvar_made")
        fln_made, frstd_made, yn_made = sem("fln_made"), sem("frstd_made"), sem("yn_made")
        logitT_made, logitT_saved, logit_made = sem("logitT_made"), sem("logitT_saved"), sem("logit_made")
        logit_saved, gap_made, gap_exp, gate_step = (
            sem("logit_saved"), sem("gap_made"), sem("gap_exp"), sem("gate_step"))
        gates_made, gateT_made, gateT_saved = sem("gates_made"), sem("gateT_made"), sem("gateT_saved")
        gate_spread, gx_made, expert_made, y_out_made = (
            sem("gate_spread"), sem("gx_made"), sem("expert_made"), sem("y_out_made"))
        passed = sem("passed")

        def wait_alone(eng, signal, count):
            eng.wait_ge(signal, count)
            eng.sem_inc(passed, 1)

        def windows(rows):
            return rows.rearrange("p (r n w) -> p n r w", r=SP, w=SP)

        def by_window(flat):
            return flat.rearrange("p (n r w) -> p n r w", r=SP, w=SP)

        def vrows(k, dr, dw):
            return vpad[:, bass.ds((k % STRIPS) * (SP * PADW) + (dr + 1) * PADW, SP * PADW)].rearrange(
                "p (r w) -> p r w", w=PADW)[:, :, dw + 1:dw + 1 + W]

        def per_row(flat):
            return flat.rearrange("p (r j) -> p r j", j=TOK)

        def over_keys(vec):
            return vec.unsqueeze(2).broadcast_to([128, UW * 4, TOK])

        MM = nc.tensor.matmul
        N_CONST_MADE = 7
        N_WEIGHT_DMAS = 1 + 7 + 8 + 2 + 12 + 4 + 6
        X_DMAS, Z_DMAS, TILE_DMAS = 5, 7, 7

        block = ctx.enter_context(nc.Block())

        @block.sync
        def _(sp):
            sp.dma_start(const_sb[:, :], consts).then_inc(const_loaded, 16)
            with nc.allow_non_contiguous_dma("small weights, once"):
                tab = bias_table.rearrange("(a b) h -> a (b h)", a=2 * SP - 1)
                for rj in range(SP):
                    for wj in range(SP):
                        j = rj * SP + wj
                        sp.dma_start(bias_all[j:j + 1, :, :].rearrange("p (r w) h -> p r (w h)", r=SP),
                                     tab[SP - 1 - rj:2 * SP - 1 - rj, (SP - 1 - wj) * HEADS:(2 * SP - 1 - wj) * HEADS]
                                     .unsqueeze(0)).then_inc(bias_loaded, 16)
                sp.wait_ge(bias_loaded, 16 * TOK)
                for k in range(1, 8):
                    sp.dma_start(bias_all[k * TOK:(k + 1) * TOK, :, :], bias_all[0:TOK, :, :]).then_inc(const_loaded, 16)
                taps = lepe_w.rearrange("(q m y) o r w -> m q y (o r w)", m=2, y=2)
                for b in range(2):
                    for g in range(4):
                        at = b * 64 + g * 16
                        sp.dma_start(lepe_sb[at:at + 16, :], taps[b, 0:8]).then_inc(const_loaded, 16)
                for half in range(2):
                    sp.dma_start(router_bias[half * E:(half + 1) * E, :],
                                 router_b.rearrange("(e o) -> e o", o=1)).then_inc(const_loaded, 16)
                sp.wait_ge(weights_cleared, 1)
                for g in range(4):
                    for part in range(3):
                        sp.dma_start(wqkv[g * CH:(g + 1) * CH, part, g * CH:(g + 1) * CH],
                                     qkv_w[part * CH:(part + 1) * CH, :].rearrange("o i -> i o")).then_inc(const_loaded, 16)
                for half in range(2):
                    rows = slice(half * C, (half + 1) * C)
                    sp.dma_start(router_sb[rows, half * E:(half + 1) * E], router_w).then_inc(const_loaded, 16)
                    sp.dma_start(expert_sb[rows, :, rows], expert_w.rearrange("e d c -> d e c")).then_inc(const_loaded, 16)
                    for part in range(3):
                        sp.dma_start(ebias_sb[part * GE + half * E:part * GE + (half + 1) * E, rows], expert_b)\
                            .then_inc(const_loaded, 16)

            x_flat = x.rearrange("b c r w -> b c (r w)")
            z_flat = z.rearrange("k b c r w -> k b c (r w)")
            z_cols = z.rearrange("k b (q m y) r w -> k b m q y (r w)", m=2, y=2)
            out_flat = out.rearrange("b c r w -> b c (r w)")

            def image(t, k, per_image):
                return t[bass.ds(k // per_image, 1)]

            def load_pair(k, ring):
                def put(rows, at, src_c, row, n):
                    sp.dma_start(xs[rows, 2 * ring:2 * ring + 2, :].rearrange("p a n -> p (a n)")[:, at * W:(at + n) * W],
                                 image(x_flat, k, IMT)[:, src_c, bass.ds(row * W, n * W)]
                                 .rearrange("b c n -> c (b n)")).then_inc(x_loaded[ring], 16)
                t = k % IMT
                put(slice(0, C), 0, slice(0, C), t * (2 * SP), 2 * SP)
                for c_to, c_from, nch in ((0, ROLL, C - ROLL), (C - ROLL, 0, ROLL)):
                    rows, src = slice(C + c_to, C + c_to + nch), slice(c_from, c_from + nch)
                    put(rows, 0, src, t * (2 * SP) + ROLL, 2 * SP - ROLL)
                    put(rows, 2 * SP - ROLL, src, (t * (2 * SP) + 2 * SP) % H, ROLL)

            load_pair(0, 0)

            def slot(s):
                ahead = s.n + 5
                if ahead % TSLOT == 0 and (s.turn is not None or ahead // TSLOT < N_TILE):
                    r = ahead // TSLOT
                    k = r if s.turn is None else s.turn * 2 + r
                    if s.turn is not None or r >= 2:
                        wait_alone(sp, k_made, (k - 1) * 2)
                    load_pair(k, r % 2)
                if st := s.strip("store_z"):
                    k, r = st
                    wait_alone(sp, fin_made, k + 1)
                    here = bass.ds((k % STRIPS) * SPX, SPX)
                    def put(roll, m, q0, q1, part):
                        sp.dma_start(image(z_cols[roll], k, STRIPS)[:, m, q0:q1, :, here]
                                     .rearrange("b q y n -> q y (b n)"), fin[part:part + 2 * (q1 - q0), r % 2, :])\
                            .then_inc(z_stored[r % 2], 16)
                    for b in range(2):
                        put(0, b, 0, 16, 64 * b)
                    put(1, 1, 0, 16, 32)
                    for half in range(2):
                        put(1, 0, half * 8 + 1, half * 8 + 8, 96 + half * 16)
                        put(1, 0, half * 8, half * 8 + 1, 96 + half * 16 + 14)
                if ti := s.tile("load_tile"):
                    k, r = ti
                    if s.turn is None:
                        last = min(2 * k + 4, N_STRIP)
                        counts = [(last + 1) // 2, last // 2]
                    else:
                        counts = [k + 2, k + 2]
                    for p in range(2):
                        wait_alone(sp, z_stored[p], counts[p] * (Z_DMAS * 16))
                    if s.later(r, 2):
                        wait_alone(sp, y_made, k - 1)
                    t = (k + 1) % IMT

                    def put(dst, rows, at, src, row, n):
                        sp.dma_start(dst[rows, r % 2, at * W:(at + n) * W],
                                     image(src, k, IMT)[:, :, bass.ds(row * W, n * W)]
                                     .rearrange("b c n -> c (b n)")).then_inc(tile_loaded[r % 2], 16)
                    for half in range(2):
                        rows = slice(half * C, (half + 1) * C)
                        put(xt, rows, 0, x_flat, t * (2 * SP) + half * SP, SP)
                        put(z0t, rows, 0, z_flat[0], t * (2 * SP) + half * SP, SP)
                    put(z2t, slice(0, C), 0, z_flat[1], (t * (2 * SP) + H - ROLL) % H, ROLL)
                    put(z2t, slice(0, C), ROLL, z_flat[1], t * (2 * SP), SP - ROLL)
                    put(z2t, slice(C, 2 * C), 0, z_flat[1], t * (2 * SP) + SP - ROLL, SP)
                if ti := s.tile("tile_out"):
                    k, r = ti
                    wait_alone(sp, y_out_made, k + 1)
                    t = (k + 1) % IMT
                    for half in range(2):
                        sp.dma_start(image(out_flat, k, IMT)[:, :, bass.ds((t * (2 * SP) + half * SP) * W, SPX)]
                                     .rearrange("b c n -> c (b n)"), y_out[half * C:(half + 1) * C, r % 2, :])\
                            .then_inc(out_stored[r % 2], 16)

            pipeline(sp, slot)
            for p in range(2):
                sp.wait_ge(out_stored[p], N_TILE // 2 * 32)

        @block.gpsimd
        def _(pool):
            G = nc.gpsimd
            for buf in (wqkv[:, :, :].rearrange("p a b -> p (a b)"), router_sb[:, :],
                        expert_sb[:, :, :].rearrange("p a b -> p (a b)"), ebias_sb[:, :]):
                G.memset(buf, 0.0).then_inc(const_step, 1)
            pool.wait_ge(const_step, 4)
            pool.sem_inc(weights_cleared, 1)
            pool.wait_ge(const_loaded, 16 * N_WEIGHT_DMAS)

            def spread(dst, src, mask):
                shape = [128, UW, 8, TOK]
                return G.tensor_tensor(dst.rearrange("p n (k i) -> p n k i", i=TOK),
                                       src.rearrange("p (n i) -> p n i", i=TOK).unsqueeze(2).broadcast_to(shape),
                                       mask.unsqueeze(1).unsqueeze(3).broadcast_to(shape), ALU.mult)

            def slot(s):
                if u := s.unit("total"):
                    n, r = u
                    pool.wait_ge(inv_made, n + 1)
                    pv = per_row(prob[:, r % 2, :])
                    G.tensor_tensor(pv, pv, over_keys(row_inv[:, r % 2, :]), ALU.mult).then_inc(prob_made, 1)
                if u := s.unit("mask_q"):
                    n, r = u
                    k, kr, j = s.in_strip("mask_q")
                    pool.wait_ge(q_saved, k + 1)
                    if s.later(r, 2):
                        pool.wait_ge(score_made, n - 1)
                    spread(qx[:, r % 2, :, :], q_sb[:, kr % 2, j * UPX:(j + 1) * UPX], const("mask_q")).then_inc(qx_made, 1)
                if u := s.unit("mask_v"):
                    n, r = u
                    k, kr, j = s.in_strip("mask_v")
                    pool.wait_ge(v_copied, k + 1)
                    if s.later(r, 2):
                        pool.wait_ge(vT_made, (n - 1) * 2)
                    spread(vx[:, r % 2, :, :], v_sb[:, kr % 2, j * UPX:(j + 1) * UPX], const("mask_v")).then_inc(vx_made, 1)
                if st := s.in_strip("pool_taps"):
                    k, kr, j = st
                    acc = lepe_p[:, kr % 2, :].rearrange("p (r w) -> p r w", w=W)
                    tmp = tap_sb[:, :].rearrange("p (r w) -> p r w", w=W)
                    if j == 0:
                        pool.wait_ge(v_saved, k + 1)
                        if s.later(r, 2):
                            pool.wait_ge(lepe_step, (k - 1) * (9 - POOL_TAPS))
                    elif r or j == 2:
                        pool.wait_ge(pool_lepe_made, k * (POOL_TAPS - 1) + (j - 1))
                    G.tensor_tensor(acc if j == 0 else tmp, vrows(k, -1, j - 1),
                                    lepe_sb[:, j:j + 1].unsqueeze(2).broadcast_to([128, SP, W]),
                                    ALU.mult).then_inc(pool_tap, 1)
                    if j:
                        pool.wait_ge(pool_tap, k * UNITS + (j + 1))
                        G.tensor_tensor(acc, acc, tmp, ALU.add).then_inc(pool_lepe_made, 1)

            pipeline(pool, slot)

        @block.tensor
        def _(pe):
            pe.wait_ge(const_loaded, 16 * N_WEIGHT_DMAS)
            pe.wait_ge(const_made, N_CONST_MADE)

            def turn_half(u, t):
                n, r = u
                pe.wait_ge(vx_made, n + 1)
                if t or r > 0:
                    pe.wait_ge(vt_saved, n * 2 + t)
                for w in range(4):
                    last = nc.tensor.transpose(bank_t[:, w * 128:(w + 1) * 128], vx[:, r % 2, 4 * t + w, :], const("ident"))
                last.then_inc(vT_made, 1)

            def slot(s):
                ex = s.in_tile("experts")
                places = [None, None]
                if ex:
                    places = [EXPERT_AT.get((ex[2], place)) for place in range(2)]

                def spread_gate(place):
                    e = places[place]
                    if e is None:
                        return
                    k, r, _ = ex
                    if e == 0:
                        pe.wait_ge(gateT_saved, k + 1)
                        if s.later(r, 1):
                            pe.wait_ge(y_out_made, k)
                        for part in range(3):
                            MM(bank_f[:, 0:SPX], ebias_part[:, part, :], gateT[:, r % 2, :], start=(part == 0), stop=False)
                    if r * E + e >= 1:
                        pe.wait_ge(gx_made, k * E + e)
                    MM(bank_g[:, 0:SPX], expert_sel[:, e, :], gateT[:, r % 2, :], start=True, stop=True)\
                        .then_inc(gate_spread, 1)

                def expert(place):
                    e = places[place]
                    if e is None:
                        return
                    k, r, _ = ex
                    pe.wait_ge(gx_made, k * E + (e + 1))
                    MM(bank_f[:, 0:SPX], expert_sb[:, e, :], gx[:, e % 2, :], start=False, stop=(e == E - 1))\
                        .then_inc(expert_made, 1)

                spread_gate(0)
                if u := s.unit("score"):
                    n, r = u
                    k, kr, j = s.in_strip("score")
                    pe.wait_ge(kx_made, k * 4 + 4)
                    pe.wait_ge(qx_made, n + 1)
                    if s.later(r, 2):
                        pe.wait_ge(shifted, n - 1)
                    MM(bank_s[r % 2][:, :], bias_hi_mid[:, :], key_sel[:, :], start=True, stop=False)
                    MM(bank_s[r % 2][:, :], bias_lo[:, :], key_sel[0:64, :], start=False, stop=False)
                    for w in range(UW):
                        last = MM(bank_s[r % 2][:, w * KEYS:(w + 1) * KEYS], qx[:, r % 2, w, :],
                                  kx[:, kr % 2, j * UW + w, :], start=False, stop=(w == UW - 1))
                    last.then_inc(score_made, 1)
                if st := s.strip("query_key"):
                    k, r = st
                    pe.wait_ge(xn_made, k + 1)
                    pe.wait_ge(v_saved, k + 1)
                    if ti := s.tile("save_gates"):
                        pe.wait_ge(gateT_saved, ti[0] + 1)
                    MM(bank_p[0][:, 0:SPX], wqkv[:, 0, :], xs[:, r % 4, :], start=True, stop=True).then_inc(q_made, 1)
                if st := s.strip("variance"):
                    k, r = st
                    pe.wait_ge(sq_made, k + 1)
                    if ti := s.tile("tile_variance"):
                        pe.wait_ge(fsq_made, ti[0] + 1)
                    if ti := s.tile("gates"):
                        pe.wait_ge(logit_saved, ti[0] + 1)
                    if s.later(r, 1):
                        pe.wait_ge(kx_made, k * 4)
                    MM(bank_p[1][:, 0:SPX], const("mean"), sq[:, r % 2, :], start=True, stop=True).then_inc(var_made, 1)
                if st := s.strip("value"):
                    k, r = st
                    pe.wait_ge(xn_made, k + 1)
                    if ti := s.tile("router"):
                        pe.wait_ge(fln_made, ti[0] + 1)
                    MM(bank_p[0][:, 0:SPX], wv[:, :], xs[:, r % 4, :], start=True, stop=True).then_inc(v_made, 1)
                if u := s.unit("turn_v"):
                    turn_half(u, 0)
                if st := s.strip("query_key"):
                    k, r = st
                    if ti := s.tile("logits"):
                        pe.wait_ge(logitT_saved, ti[0] + 1)
                    pe.wait_ge(ln_made, k + 1)
                    MM(bank_p[1][:, 0:SPX], wqkv[:, 1, :], xs[:, r % 4, :], start=True, stop=True).then_inc(k_made, 1)
                expert(0)
                spread_gate(1)
                if u := s.unit("turn_v"):
                    turn_half(u, 1)
                if st := s.strip("centre"):
                    k, r = st
                    pe.wait_ge(x_loaded[r // 2 % 2], (k // 4 + 1) * (X_DMAS * 16))
                    if s.later(r, 1):
                        pe.wait_ge(q_saved, k)
                    MM(bank_p[0][:, 0:SPX], const("centre"), xs[:, r % 4, :], start=True, stop=True).then_inc(xc_made, 1)
                if ti := s.tile("tile_sum"):
                    k, r = ti
                    pe.wait_ge(y_made, k + 1)
                    pe.wait_ge(kx_made, strips_to(s, 2 * k + 8) * 4)
                    MM(bank_p[1][:, 0:SPX], const("centre"), y[:, r % 2, :], start=True, stop=True).then_inc(fc_made, 1)
                if ti := s.tile("tile_variance"):
                    k, r = ti
                    pe.wait_ge(fsq_made, k + 1)
                    pe.wait_ge(q_saved, strips_to(s, 2 * k + 8))
                    pe.wait_ge(sq_made, strips_to(s, 2 * k + 9))
                    MM(bank_p[0][:, 0:SPX], const("mean"), ysq[:, :], start=True, stop=True).then_inc(fvar_made, 1)
                if ti := s.tile("router"):
                    k, r = ti
                    pe.wait_ge(yn_made, k + 1)
                    pe.wait_ge(ln_made, strips_to(s, 2 * k + 9))
                    MM(bank_p[1][0:GE, 0:SPX], router_sb[:, :], yn[:, r % 2, :], start=True, stop=True)\
                        .then_inc(logitT_made, 1)
                if ti := s.tile("logits"):
                    k, r = ti
                    pe.wait_ge(kx_made, strips_to(s, 2 * k + 9) * 4)
                    wait_alone(pe, logitT_saved, k + 1)
                    for blk in range(TBLK):
                        last = nc.tensor.transpose(bank_p[1][:, blk * GE:(blk + 1) * GE],
                                                   logitT[:, blk * 128:(blk + 1) * 128], const("ident", GE)[:, 0:GE])
                    last.then_inc(logit_made, 1)
                if u := s.unit("product"):
                    n, r = u
                    pe.wait_ge(probT_made, n + 1)
                    pe.wait_ge(vt_saved, (n + 1) * 2)
                    if s.later(r, 1):
                        pe.wait_ge(picked, n * 2)
                    for w in range(UW):
                        for b in range(2):
                            last = MM(bank_o[64 * b:64 * b + 64, w * 32:(w + 1) * 32], vt[:, r % 2, w, 64 * b:64 * b + 64],
                                      probT[:, r % 2, w, b * 32:(b + 1) * 32], start=True, stop=True)
                    last.then_inc(pv_made, 1)
                expert(1)
                if ti := s.tile("turn_gates"):
                    k, r = ti
                    pe.wait_ge(v_saved, strips_to(s, 2 * k + 10))
                    pe.wait_ge(gates_made, k + 1)
                    for blk in range(TBLK):
                        last = MM(bank_p[0][0:3 * GE, blk * 128:(blk + 1) * 128],
                                  gate_part[:, blk, :, :].rearrange("p a b -> p (a b)"), ident_bf[:, :],
                                  start=True, stop=True)
                    last.then_inc(gateT_made, 1)

            pipeline(pe, slot)

        @block.scalar
        def _(act):
            S = nc.scalar
            S.preload_act_table_set("natural_log_exp_and_others")
            act.wait_ge(const_loaded, 16 * N_WEIGHT_DMAS)
            S.activation(key_sel[:, :].rearrange("p (n k) -> p n k", k=KEYS),
                         const("ident64x2").unsqueeze(1).broadcast_to([128, UW, KEYS]), ACT.Copy).then_inc(const_made, 1)
            S.activation(expert_sel[:, :, :].rearrange("p e n -> p (e n)"), const("expert_sel", 3 * GE),
                         ACT.Copy).then_inc(const_made, 1)
            S.activation(ident_bf[:, :], const("ident"), ACT.Copy).then_inc(const_made, 1)
            act.wait_ge(const_made, N_CONST_MADE)

            def save_vt(u, t):
                n, r = u
                act.wait_ge(vT_made, n * 2 + (t + 1))
                S.activation(vt[:, r % 2, 4 * t:4 * t + 4, :].rearrange("p n k -> p (n k)"), bank_t[:, :],
                             ACT.Copy).then_inc(vt_saved, 1)

            def slot(s):
                if ti := s.tile("save_gates"):
                    k, r = ti
                    act.wait_ge(gateT_made, k + 1)
                    S.activation(gateT[:, r % 2, :], bank_p[0][0:3 * GE, 0:SPX], ACT.Copy).then_inc(gateT_saved, 1)
                if st := s.strip("query_key"):
                    k, r = st
                    act.wait_ge(q_made, k + 1)
                    S.activation(by_window(q_sb[:, r % 2, :]), windows(bank_p[0][:, 0:SPX]), ACT.Copy,
                                 scale=float(HD) ** -0.5).then_inc(q_saved, 1)
                if st := s.strip("variance"):
                    k, r = st
                    act.wait_ge(var_made, k + 1)
                    S.activation(rstd[:, r % 2, :], bank_p[1][:, 0:SPX], ACT.Ln, bias=const("eps1")).then_inc(ln_made, 1)
                if st := s.strip("value"):
                    k, r = st
                    act.wait_ge(v_made, k + 1)
                    S.activation(vrows(k, 0, 0), bank_p[0][:, 0:SPX].rearrange("p (r w) -> p r w", w=W),
                                 ACT.Copy).then_inc(v_saved, 1)
                if ti := s.tile("turn_gates"):
                    act.wait_ge(gap_made, ti[0] + 1)
                    S.activation(gate_vec[:, 2, :], gate_vec[:, 2, :], ACT.Exp).then_inc(gap_exp, 1)
                if u := s.unit("turn_v"):
                    save_vt(u, 0)
                if st := s.strip("variance"):
                    k, r = st
                    act.wait_ge(ln_made, k + 1)
                    S.activation(rstd[:, r % 2, :], rstd[:, r % 2, :], ACT.Exp, scale=-0.5).then_inc(rstd_made, 1)
                if u := s.unit("score"):
                    n, r = u
                    act.wait_ge(shifted, n + 1)
                    S.activation(prob[:, r % 2, :], prob[:, r % 2, :], ACT.Exp).then_inc(exp_made, 1)
                if st := s.strip("query_key"):
                    k, r = st
                    act.wait_ge(k_made, k + 1)
                    for m in range(4):
                        S.activation(kx[:, r % 2, :, m * TOK:(m + 1) * TOK].rearrange("p n (r w) -> p n r w", w=SP),
                                     windows(bank_p[1][:, 0:SPX]), ACT.Copy,
                                     scale=const("mask_k")[:, m:m + 1]).then_inc(kx_made, 1)
                if u := s.unit("turn_v"):
                    save_vt(u, 1)
                if st := s.strip("centre"):
                    k, r = st
                    act.wait_ge(xc_made, k + 1)
                    S.activation(xs[:, r % 4, :], bank_p[0][:, 0:SPX], ACT.Copy).then_inc(xc_saved, 1)
                    S.activation(sq[:, r % 2, :], bank_p[0][:, 0:SPX], ACT.Square).then_inc(sq_made, 1)
                if st := s.strip("copy_v"):
                    k, r = st
                    S.activation(by_window(v_sb[:, r % 2, :]),
                                 vrows(k, 0, 0).rearrange("p r (n w) -> p n r w", w=SP), ACT.Copy).then_inc(v_copied, 1)
                if ti := s.tile("tile_sum"):
                    k, r = ti
                    act.wait_ge(fc_made, k + 1)
                    S.activation(yn[:, r % 2, :], bank_p[1][:, 0:SPX], ACT.Copy).then_inc(fc_saved, 1)
                    S.activation(ysq[:, :], bank_p[1][:, 0:SPX], ACT.Square).then_inc(fsq_made, 1)
                if ti := s.tile("tile_variance"):
                    k, r = ti
                    act.wait_ge(fvar_made, k + 1)
                    S.activation(yrstd[:, :], bank_p[0][:, 0:SPX], ACT.Ln, bias=const("eps2")).then_inc(fln_made, 1)
                    act.wait_ge(fln_made, k + 1)
                    S.activation(yrstd[:, :], yrstd[:, :], ACT.Exp, scale=-0.5).then_inc(frstd_made, 1)
                if ti := s.tile("router"):
                    k, r = ti
                    act.wait_ge(logitT_made, k + 1)
                    S.activation(logitT[:, :], bank_p[1][0:GE, 0:SPX], ACT.Identity,
                                 bias=router_bias[:, :]).then_inc(logitT_saved, 1)

            pipeline(act, slot)

        @block.vector
        def _(dve):
            V = nc.vector
            V.memset(vpad[:, :], 0.0).then_inc(const_made, 1)
            dve.wait_ge(const_loaded, 16 * N_WEIGHT_DMAS)
            step = [4]

            def chained(ins):
                step[0] += 1
                ins.then_inc(const_step, 1)
                dve.wait_ge(const_step, step[0])

            for b in range(2):
                last = V.tensor_copy(wv[:, 64 * b:64 * b + 64].rearrange("p (q y) -> p q y", y=2),
                                     wqkv[:, 2, :].rearrange("p (q m y) -> p q m y", m=2, y=2)[:, :, b, :])
            last.then_inc(const_made, 1)
            by_head = bias_all[:, :, :].rearrange("p i (A m) -> p (i A) m", A=2)
            chained(V.tensor_tensor(by_head, by_head, const("mask_b").unsqueeze(1).broadcast_to([128, 2 * TOK, 4]),
                                    ALU.mult))
            chained(V.tensor_reduce(bias_sb[:, :].rearrange("p (A i) -> p i A", A=2),
                                    bias_all[:, :, :].rearrange("p i (A m) -> p i A m", A=2), AX.X, ALU.add))

            def cut(part, rest, whole):
                for k in range(3):
                    chained(V.tensor_copy(part[:, k, :], whole))
                    if k < 2:
                        chained(V.tensor_tensor(rest[:, k, :], whole, part[:, k, :], ALU.subtract))
                        whole = rest[:, k, :]

            cut(bias_part, bias_rest, bias_sb[:, :])
            cut(ebias_part, ebias_rest, ebias_sb[:, :])
            dve.sem_inc(const_made, 1)
            for dst, rows, k in ((bias_hi_mid, slice(0, 64), 0), (bias_hi_mid, slice(64, 128), 1),
                                 (bias_lo, slice(0, 64), 2)):
                last = V.tensor_copy(dst[rows, :].rearrange("p (g a) -> p g a", g=4),
                                     bias_part[rows, k, :].unsqueeze(1).broadcast_to([64, 4, 2 * TOK]))
            last.then_inc(const_made, 1)

            GT = TBLK * 2

            def per_e(v):
                return v.rearrange("p (t e) -> p t e", e=E)

            def wide(vec):
                return vec.unsqueeze(2).broadcast_to([128, GT, E])

            def by_block(flat):
                return flat.rearrange("p (t a) -> p t a", a=GE)

            rank = const("rank").unsqueeze(1).broadcast_to([128, GT, E])
            one1, one2, tmp, rest2, gates, left1, left2 = (gate_tmp[:, k, :] for k in range(7))
            best1, best2, gap, vec, total, inv = (gate_vec[:, k, :] for k in range(6))

            def part(k):
                return gate_part[:, :, k, :]

            GATE_SPLIT, GATE_STEPS = 12, 22

            def gate_step_of(k, at):
                if at == 0:
                    dve.wait_ge(logit_saved, k + 1)
                elif at == GATE_SPLIT:
                    dve.wait_ge(gap_exp, k + 1)
                else:
                    dve.wait_ge(gate_step, k * (GATE_STEPS - 2) + (at if at < GATE_SPLIT else at - 1))
                best, src, hot = (best1, logits[:, :], one1) if at < 6 else (best2, rest2, one2)
                choice = at if at < 5 else at - 6
                if choice == 0:
                    done = V.tensor_reduce(best, per_e(src), AX.X, ALU.max)
                elif choice == 1:
                    done = V.tensor_tensor(per_e(tmp), per_e(src), wide(best), ALU.is_equal)
                elif choice == 2:
                    done = V.tensor_tensor(per_e(tmp), per_e(tmp), rank, ALU.mult)
                elif choice == 3:
                    done = V.tensor_reduce(vec, per_e(tmp), AX.X, ALU.max)
                elif choice == 4:
                    done = V.tensor_tensor(per_e(hot), per_e(tmp), wide(vec), ALU.is_equal)
                elif at == 5:
                    done = V.scalar_tensor_tensor(rest2, one1, -3.0e38, logits[:, :], ALU.mult, ALU.add)
                elif at == 11:
                    done = V.tensor_tensor(gap, best2, best1, ALU.subtract)
                elif at == 12:
                    done = V.tensor_scalar(total, gap, 1.0, None, ALU.add)
                elif at == 13:
                    done = V.reciprocal(inv, total)
                elif at == 14:
                    done = V.tensor_tensor(per_e(gates), per_e(one2), wide(gap), ALU.mult)
                elif at == 15:
                    done = V.tensor_tensor(gates, gates, one1, ALU.add)
                elif at == 16:
                    done = V.tensor_tensor(per_e(gates), per_e(gates), wide(inv), ALU.mult)
                elif at == 17:
                    done = V.tensor_copy(part(0), by_block(gates))
                elif at == 18:
                    done = V.tensor_tensor(by_block(left1), by_block(gates), part(0), ALU.subtract)
                elif at == 19:
                    done = V.tensor_copy(part(1), by_block(left1))
                elif at == 20:
                    done = V.tensor_tensor(by_block(left2), by_block(left1), part(1), ALU.subtract)
                else:
                    done = V.tensor_copy(part(2), by_block(left2))
                done.then_inc(gap_made if at == 11 else gates_made if at == 21 else gate_step, 1)

            def slot(s):
                ti = s.tile("gates")
                late = s.tile("turn_gates")

                def gate_work(first, last=None):
                    for at in range(first, (first if last is None else last) + 1):
                        if ti and at < GATE_SPLIT:
                            gate_step_of(ti[0], at)
                        if late and GATE_SPLIT + at < GATE_STEPS:
                            gate_step_of(late[0], GATE_SPLIT + at)

                ex = s.in_tile("experts")

                def gate_product(place):
                    e = ex and EXPERT_AT.get((ex[2], place))
                    if e is None:
                        return
                    k, r, _ = ex
                    dve.wait_ge(gate_spread, k * E + (e + 1))
                    if r * E + e >= 2:
                        dve.wait_ge(expert_made, k * E + e - 1)
                    V.tensor_tensor(gx[:, e % 2, :], bank_g[:, 0:SPX], yn[:, r % 2, :], ALU.mult).then_inc(gx_made, 1)

                def tap(k, r, j):
                    acc = lepe[:, r % 2, :].rearrange("p (r w) -> p r w", w=W)
                    first = lepe_p[:, r % 2, :].rearrange("p (r w) -> p r w", w=W)
                    if j == 0:
                        dve.wait_ge(v_saved, strips_to(s, k + 2))
                        dve.wait_ge(pool_lepe_made, (k + 1) * (POOL_TAPS - 1))
                    else:
                        dve.wait_ge(lepe_step, k * (9 - POOL_TAPS) + j)
                    t = POOL_TAPS + j
                    V.scalar_tensor_tensor(acc, vrows(k, t // 3 - 1, t % 3 - 1), lepe_sb[:, t:t + 1],
                                           first if j == 0 else acc, ALU.mult, ALU.add).then_inc(lepe_step, 1)

                if ti:
                    k, r = ti
                    dve.wait_ge(logit_made, k + 1)
                    V.tensor_copy(logits[:, :], bank_p[1][:, 0:TBLK * GE]).then_inc(logit_saved, 1)
                if u := s.unit("total"):
                    n, r = u
                    dve.wait_ge(exp_made, n + 1)
                    V.tensor_reduce(row_sum[:, r % 2, :], per_row(prob[:, r % 2, :]), AX.X, ALU.add).then_inc(sum_made, 1)
                gate_work(0)
                pick = s.unit("pick")
                if pick:
                    n, r = pick
                    k, kr, j = s.in_strip("pick")
                    dve.wait_ge(pv_made, n + 1)
                    pv = bank_o[:, 0:UW * 32].rearrange("p (n m i) -> p m n i", m=2, i=TOK)
                    acc = att[:, kr % 2, j * UPX:(j + 1) * UPX].rearrange("p (n i) -> p n i", i=TOK)
                    V.tensor_scalar(acc, pv[:, 0], const("mask_o")[:, 0:1], None, ALU.mult).then_inc(picked, 1)
                if u := s.unit("total"):
                    n, r = u
                    dve.wait_ge(sum_made, n + 1)
                    V.reciprocal(row_inv[:, r % 2, :], row_sum[:, r % 2, :]).then_inc(inv_made, 1)
                gate_work(1)
                if yt := s.tile("router"):
                    k, r = yt
                    dve.wait_ge(frstd_made, k + 1)
                    V.tensor_tensor(yn[:, r % 2, :], yn[:, r % 2, :], yrstd[:, :], ALU.mult).then_inc(yn_made, 1)
                if yt := s.tile("tile_sum"):
                    k, r = yt
                    dve.wait_ge(tile_loaded[r % 2], (k // 2 + 1) * (TILE_DMAS * 16))
                    if s.later(r, 2):
                        dve.wait_ge(y_out_made, k - 1)
                    V.tensor_tensor(y[:, r % 2, :], xt[:, r % 2, :], z0t[:, r % 2, :], ALU.add).then_inc(y_step, 1)
                if u := s.unit("turn_p"):
                    n, r = u
                    dve.wait_ge(prob_made, n + 1)
                    V.transpose(probT[:, r % 2, :, :].rearrange("p n k -> p (n k)"), prob[:, r % 2, :]).then_inc(probT_made, 1)
                gate_work(2)
                if pick:
                    dve.wait_ge(picked, n_picked(pick) * 2 + 1)
                    V.scalar_tensor_tensor(acc, pv[:, 1], const("mask_o")[:, 1:2], acc, ALU.mult, ALU.add).then_inc(picked, 1)
                gate_work(3)
                if u := s.unit("score"):
                    n, r = u
                    dve.wait_ge(score_made, n + 1)
                    V.tensor_reduce(row_max[:, r % 2, :], per_row(bank_s[r % 2][:, :]), AX.X, ALU.max).then_inc(max_made, 1)
                gate_work(4)
                gate_product(0)
                if yt := s.tile("tile_sum"):
                    k, r = yt
                    dve.wait_ge(y_step, k + 1)
                    V.tensor_tensor(y[:, r % 2, :], y[:, r % 2, :], z2t[:, r % 2, :], ALU.add).then_inc(y_made, 1)
                taps = s.in_strip("taps")
                gate_work(5)
                if taps and not ex_here(ex, 0):
                    tap(taps[0], taps[1], 2 * taps[2])
                if u := s.unit("score"):
                    n, r = u
                    dve.wait_ge(max_made, n + 1)
                    V.tensor_tensor(per_row(prob[:, r % 2, :]), per_row(bank_s[r % 2][:, :]),
                                    over_keys(row_max[:, r % 2, :]), ALU.subtract).then_inc(shifted, 1)
                if taps and ex_here(ex, 0):
                    tap(taps[0], taps[1], 2 * taps[2])
                gate_work(6)
                if st := s.strip("variance"):
                    k, r = st
                    dve.wait_ge(rstd_made, k + 1)
                    V.tensor_tensor(xs[:, r % 4, :], xs[:, r % 4, :], rstd[:, r % 2, :], ALU.mult).then_inc(xn_made, 1)
                if taps:
                    tap(taps[0], taps[1], 2 * taps[2] + 1)
                gate_work(7, 11)
                gate_product(1)
                if st := s.strip("add_taps"):
                    k, r = st
                    if s.later(r, 2):
                        dve.wait_ge(z_stored[r % 2], k // 2 * (Z_DMAS * 16))
                    dve.wait_ge(lepe_step, (k + 1) * (9 - POOL_TAPS))
                    dve.wait_ge(picked, (k + 1) * (2 * UNITS))
                    V.tensor_tensor(windows(fin[:, r % 2, :]), by_window(att[:, r % 2, :]),
                                    windows(lepe[:, r % 2, :]), ALU.add).then_inc(fin_made, 1)
                if yt := s.tile("tile_out"):
                    k, r = yt
                    dve.wait_ge(expert_made, (k + 1) * E)
                    if s.later(r, 2):
                        dve.wait_ge(out_stored[r % 2], k // 2 * 32)
                    V.tensor_tensor(y_out[:, r % 2, :], bank_f[:, 0:SPX], y[:, r % 2, :], ALU.add).then_inc(y_out_made, 1)

            def ex_here(ex, place):
                return bool(ex) and (ex[2], place) in EXPERT_AT

            def n_picked(pick):
                return pick[0]

            pipeline(dve, slot)


_INS = ["x", "L0_conv_qkv_w", "L0_conv_lepe_w", "L0_conv_bias_table", "L0_ffn_router_w", "L0_ffn_router_b",
        "L0_ffn_expert_w", "L0_ffn_expert_b"]


def kernel(**inputs):
    import numpy as _np
    import concourse.bacc as _bacc
    from concourse import mybir as _mybir
    from concourse.bass_utils import run_bass_kernel_spmd as _run

    nc = _bacc.Bacc("TRN2", target_bir_lowering=False, num_devices=1)
    arrays, args = {}, []
    for name in _INS:
        arrays[f"in_{name}"] = _np.ascontiguousarray(inputs[name])
    arrays["in_constants"] = CONSTS
    for name, a in arrays.items():
        args.append(nc.dram_tensor(name, a.shape, _mybir.dt.from_np(a.dtype), kind="ExternalInput").ap())
    args.append(nc.dram_tensor("out_y", (B, C, H, W), _mybir.dt.float32, kind="ExternalOutput").ap())
    metaformer_block(nc, *args)
    r = _run(nc, [arrays], core_ids=[0])
    return r.results[0]["out_y"]
```

```python
from contextlib import ExitStack

import numpy as np
import concourse.bass as bass
from concourse import mybir

FP32 = mybir.dt.float32
BF16 = mybir.dt.bfloat16
ALU = mybir.AluOpType
ACT = mybir.ActivationFunctionType
AX = mybir.AxisListType

B, C, H, W = 8, 64, 96, 96
CH = C // 2
HEADS, HD = 8, 4
SP = 4
TOK = SP * SP
E = 8
ROLL = 2
STRIPS = H // SP
SPX = SP * W
WIN = W // SP
UW = 8
UNITS = WIN // UW
UPX = UW * TOK
KEYS = 4 * TOK
UK = UW * KEYS
PADW = W + 2
TSLOT = 2 * UNITS
TBLK = SPX // 128
GE = 2 * E
N_UNIT, N_STRIP, N_TILE = B * STRIPS * UNITS, B * STRIPS, B * STRIPS // 2
IMT = STRIPS // 2
LN1_EPS, LN2_EPS = 1e-6, 1e-5
POOL_TAPS = 3

LAG = dict(
    centre=0, variance=1, value=2, query_key=3,
    mask_q=5, place_bias=5, score=6, shift=7, total=8,
    mask_v=8, turn_p=9, turn_v=9, product=10, pick=11,
    copy_v=6, tap_products=6, pool_taps=7, taps=10, add_taps=13,
    store_z=13, load_tile=24, tile_sum=27, tile_variance=28, router=29, logits=30, gates=31,
    gap_exp=33, turn_gates=34, experts=35, tile_out=39)
PERIOD = 2 * TSLOT
DEPTH = LAG["tile_out"]
HEAD = -(-DEPTH // PERIOD) * PERIOD
EXPERT_AT = {(0, 0): 0, (0, 1): 1, (1, 0): 2, (1, 1): 3, (2, 0): 4, (2, 1): 5, (3, 0): 6, (3, 1): 7}


class Slot:

    def __init__(self, number, turn=None):
        self.n, self.turn = number, turn

    def _item(self, lag, span, total):
        at = self.n - LAG[lag]
        if self.turn is None and not 0 <= at // span < total:
            return None
        k = at // span
        return (k if self.turn is None else self.turn * (PERIOD // span) + k), k

    def unit(self, lag):
        return self._item(lag, 1, N_UNIT)

    def strip(self, lag):
        return self._item(lag, UNITS, N_STRIP) if (self.n - LAG[lag]) % UNITS == 0 else None

    def in_strip(self, lag):
        got = self._item(lag, UNITS, N_STRIP)
        return got and (*got, (self.n - LAG[lag]) % UNITS)

    def tile(self, lag):
        return self._item(lag, TSLOT, N_TILE) if (self.n - LAG[lag]) % TSLOT == 0 else None

    def in_tile(self, lag):
        got = self._item(lag, TSLOT, N_TILE)
        return got and (*got, (self.n - LAG[lag]) % TSLOT)

    def later(self, residue, least):
        assert self.turn is None or residue >= least
        return residue >= least


def strips_to(s, count):
    return min(count, N_STRIP) if s.turn is None else count


def pipeline(eng, body):
    turns = (N_UNIT - HEAD) // PERIOD - 1
    for n in range(HEAD):
        body(Slot(n))
    with eng.Fori(0, turns) as turn:
        for n in range(HEAD, HEAD + PERIOD):
            body(Slot(n, turn))
    for n in range(HEAD + turns * PERIOD, N_UNIT + DEPTH + 1):
        body(Slot(n))




def _constants():
    p = np.arange(128)
    g, c = p // CH, p % CH
    head = c % HEADS
    vg, vx, vbeta = p // 16 % 4, p // 2 % 8, p % 2
    same64 = (p[:, None] // C == p[None, :] // C).astype(np.float32)
    parts = {
        "ident": np.eye(128),
        "centre": np.eye(128) - same64 / C,
        "mean": same64 / C,
        "mask_q": (g[:, None] == p[None, :8] // 2) & ((head >> 2)[:, None] == p[None, :8] % 2),
        "mask_k": (head & 3)[:, None] == p[None, :4],
        "mask_v": (vg[:, None] == p[None, :8] // 2) & (vbeta[:, None] == p[None, :8] % 2),
        "mask_o": (vx & 1)[:, None] == p[None, :2],
        "mask_b": (p[:, None] // TOK % 4) == p[None, :4],
        "expert_sel": np.stack([(p[:, None] % E == e) & (p[:, None] // E % 2 == p[None, :] // C)
                                & (p[:, None] < 3 * GE) for e in range(E)], axis=1).reshape(128, E * 128),
        "rank": np.tile(E - np.arange(E), (128, 1)),
        "eps1": np.full((128, 1), LN1_EPS),
        "eps2": np.full((128, 1), LN2_EPS),
    }
    at, cols = {}, 0
    for name, a in parts.items():
        at[name] = (cols, a.shape[1])
        cols += a.shape[1]
    return at, np.concatenate([a.astype(np.float32) for a in parts.values()], axis=1)


CONST_AT, CONSTS = _constants()


def metaformer_block(nc, x, qkv_w, lepe_w, bias_table, router_w, router_b, expert_w, expert_b, consts, out):
    ctx = ExitStack()
    with ctx:
        def sb(name, shape, dt=FP32):
            return ctx.enter_context(nc.sbuf_tensor(name, shape, dt))

        def sem(name):
            return ctx.enter_context(nc.semaphore(name))

        def sems(name):
            return [sem(name + "0"), sem(name + "1")]

        z = nc.dram_tensor("z", [2, B, C, H, W], FP32, kind="Internal").ap()

        const_sb = sb("const_sb", [128, CONSTS.shape[1]])

        def const(name, rows=128):
            at, n = CONST_AT[name]
            return const_sb[0:rows, at:at + n]

        wqkv = sb("wqkv", [128, 3, 128])
        wv = sb("wv", [128, 128])
        lepe_sb = sb("lepe_sb", [128, 9])
        bias_all = sb("bias_all", [KEYS, TOK, HEADS])
        bias_sb = sb("bias_sb", [KEYS, 4, 2 * TOK])
        bias_tile = sb("bias_tile", [128, UW, KEYS])
        router_sb = sb("router_sb", [128, GE])
        router_bias = sb("router_bias", [GE, 1])
        expert_sb = sb("expert_sb", [128, E, 128])
        expert_sel = sb("expert_sel", [3 * GE, E, 128], BF16)
        ebias_sb = sb("ebias_sb", [3 * GE, 128])
        ebias_rest = sb("ebias_rest", [3 * GE, 2, 128])
        ebias_part = sb("ebias_part", [3 * GE, 3, 128], BF16)
        ident_bf = sb("ident_bf", [128, 128], BF16)

        xs = sb("xs", [128, 4, SPX])
        vpad = sb("vpad", [128, (H + 2) * PADW])
        sq = sb("sq", [128, 2, SPX])
        rstd = sb("rstd", [128, 2, SPX])
        q_sb = sb("q_sb", [128, 2, SPX])
        v_sb = sb("v_sb", [128, 2, SPX])
        qx = sb("qx", [128, 2, UW, 128])
        kx = sb("kx", [128, 2, WIN, KEYS])
        vx = sb("vx", [128, 2, UW, 128])
        vt = sb("vt", [128, 2, UW, 128])
        prob = sb("prob", [128, 4, UK])
        probT = sb("probT", [128, 2, UW, KEYS])
        row_max = sb("row_max", [128, 2, UW * 4])
        row_sum = sb("row_sum", [128, 2, UW * 4])
        row_inv = sb("row_inv", [128, 2, UW * 4])
        att = sb("att", [128, 2, SPX])
        tap_sb = sb("tap_sb", [128, POOL_TAPS - 1, SPX])
        lepe_p = sb("lepe_p", [128, 2, SPX])
        lepe = sb("lepe", [128, 2, SPX])
        fin = sb("fin", [128, 2, SPX])
        xt = sb("xt", [128, 2, SPX])
        z0t = sb("z0t", [128, 2, SPX])
        z2t = sb("z2t", [128, 2, SPX])
        y = sb("y", [128, 2, SPX])
        yn = sb("yn", [128, 2, SPX])
        ysq = sb("ysq", [128, SPX])
        yrstd = sb("yrstd", [128, SPX])
        logitT = sb("logitT", [GE, SPX])
        logits = sb("logits", [128, TBLK * GE])
        gate_tmp = sb("gate_tmp", [128, 7, TBLK * GE])
        gate_vec = sb("gate_vec", [128, 6, TBLK * 2])
        gate_part = sb("gate_part", [128, TBLK, 3, GE], BF16)
        gateT = sb("gateT", [3 * GE, 2, SPX], BF16)
        gx = sb("gx", [128, 2, SPX])
        y_out = sb("y_out", [128, 2, SPX])

        banks = [ctx.enter_context(nc.psum_tensor(f"bank{n}", [128, 512], FP32)) for n in range(8)]
        bank_s, bank_o, bank_t, bank_p, bank_g, bank_f = banks[0:2], banks[2], banks[3], banks[4:6], banks[6], banks[7]

        bias_loaded, const_loaded, const_made, const_step = (
            sem("bias_loaded"), sem("const_loaded"), sem("const_made"), sem("const_step"))
        weights_cleared = sem("weights_cleared")
        x_loaded = sems("x_loaded")
        xc_made, xc_saved, sq_made, var_made = sem("xc_made"), sem("xc_saved"), sem("sq_made"), sem("var_made")
        ln_made, rstd_made, xn_made = sem("ln_made"), sem("rstd_made"), sem("xn_made")
        v_made, v_saved, q_made, k_made = sem("v_made"), sem("v_saved"), sem("q_made"), sem("k_made")
        q_saved, kx_made, v_copied = sem("q_saved"), sem("kx_made"), sem("v_copied")
        qx_made, vx_made = sem("qx_made"), sem("vx_made")
        bias_turned, bias_made, bias_placed = sem("bias_turned"), sem("bias_made"), sem("bias_placed")
        score_made, max_made, shifted = sem("score_made"), sem("max_made"), sem("shifted")
        exp_made, sum_made, inv_made, prob_made = sem("exp_made"), sem("sum_made"), sem("inv_made"), sem("prob_made")
        probT_made, vT_made, vt_saved = sem("probT_made"), sem("vT_made"), sem("vt_saved")
        pv_made, picked = sem("pv_made"), sem("picked")
        tap_made, pool_lepe_made, lepe_step, fin_made = (
            sem("tap_made"), sem("pool_lepe_made"), sem("lepe_step"), sem("fin_made"))
        z_stored, tile_loaded, out_stored = sems("z_stored"), sems("tile_loaded"), sems("out_stored")
        y_step, y_made = sem("y_step"), sem("y_made")
        fc_made, fc_saved, fsq_made, fvar_made = sem("fc_made"), sem("fc_saved"), sem("fsq_made"), sem("fvar_made")
        fln_made, frstd_made, yn_made = sem("fln_made"), sem("frstd_made"), sem("yn_made")
        logitT_made, logitT_saved, logit_made = sem("logitT_made"), sem("logitT_saved"), sem("logit_made")
        logit_saved, gap_made, gap_exp, gate_step = (
            sem("logit_saved"), sem("gap_made"), sem("gap_exp"), sem("gate_step"))
        gates_made, gateT_made, gateT_saved = sem("gates_made"), sem("gateT_made"), sem("gateT_saved")
        gate_spread, gx_made, expert_made, y_out_made = (
            sem("gate_spread"), sem("gx_made"), sem("expert_made"), sem("y_out_made"))
        passed = sem("passed")

        def wait_alone(eng, signal, count):
            eng.wait_ge(signal, count)
            eng.sem_inc(passed, 1)

        def windows(rows):
            return rows.rearrange("p (r n w) -> p n r w", r=SP, w=SP)

        def by_window(flat):
            return flat.rearrange("p (n r w) -> p n r w", r=SP, w=SP)

        def vrows(k, dr, dw):
            return vpad[:, bass.ds((k % STRIPS) * (SP * PADW) + (dr + 1) * PADW, SP * PADW)].rearrange(
                "p (r w) -> p r w", w=PADW)[:, :, dw + 1:dw + 1 + W]

        def per_row(flat):
            return flat.rearrange("p (r j) -> p r j", j=TOK)

        def over_keys(vec):
            return vec.unsqueeze(2).broadcast_to([128, UW * 4, TOK])

        LOGITS_AT = UW * 32
        MM = nc.tensor.matmul
        N_CONST_MADE = 6
        N_WEIGHT_DMAS = 1 + 3 + 8 + 2 + 12 + 4 + 6
        X_DMAS, Z_DMAS, TILE_DMAS = 5, 7, 7

        block = ctx.enter_context(nc.Block())

        @block.sync
        def _(sp):
            sp.dma_start(const_sb[:, :], consts).then_inc(const_loaded, 16)
            with nc.allow_non_contiguous_dma("small weights, once"):
                tab = bias_table.rearrange("(a b) h -> a (b h)", a=2 * SP - 1)
                for rj in range(SP):
                    for wj in range(SP):
                        j = rj * SP + wj
                        sp.dma_start(bias_all[j:j + 1, :, :].rearrange("p (r w) h -> p r (w h)", r=SP),
                                     tab[SP - 1 - rj:2 * SP - 1 - rj, (SP - 1 - wj) * HEADS:(2 * SP - 1 - wj) * HEADS]
                                     .unsqueeze(0)).then_inc(bias_loaded, 16)
                sp.wait_ge(bias_loaded, 16 * TOK)
                for k in range(1, 4):
                    sp.dma_start(bias_all[k * TOK:(k + 1) * TOK, :, :], bias_all[0:TOK, :, :]).then_inc(const_loaded, 16)
                taps = lepe_w.rearrange("(q m y) o r w -> m q y (o r w)", m=2, y=2)
                for b in range(2):
                    for g in range(4):
                        at = b * 64 + g * 16
                        sp.dma_start(lepe_sb[at:at + 16, :], taps[b, 0:8]).then_inc(const_loaded, 16)
                for half in range(2):
                    sp.dma_start(router_bias[half * E:(half + 1) * E, :],
                                 router_b.rearrange("(e o) -> e o", o=1)).then_inc(const_loaded, 16)
                sp.wait_ge(weights_cleared, 1)
                for g in range(4):
                    for part in range(3):
                        sp.dma_start(wqkv[g * CH:(g + 1) * CH, part, g * CH:(g + 1) * CH],
                                     qkv_w[part * CH:(part + 1) * CH, :].rearrange("o i -> i o")).then_inc(const_loaded, 16)
                for half in range(2):
                    rows = slice(half * C, (half + 1) * C)
                    sp.dma_start(router_sb[rows, half * E:(half + 1) * E], router_w).then_inc(const_loaded, 16)
                    sp.dma_start(expert_sb[rows, :, rows], expert_w.rearrange("e d c -> d e c")).then_inc(const_loaded, 16)
                    for part in range(3):
                        sp.dma_start(ebias_sb[part * GE + half * E:part * GE + (half + 1) * E, rows], expert_b)\
                            .then_inc(const_loaded, 16)

            x_flat = x.rearrange("b c r w -> b c (r w)")
            z_flat = z.rearrange("k b c r w -> k b c (r w)")
            z_cols = z.rearrange("k b (q m y) r w -> k b m q y (r w)", m=2, y=2)
            out_flat = out.rearrange("b c r w -> b c (r w)")

            def image(t, k, per_image):
                return t[bass.ds(k // per_image, 1)]

            def load_pair(k, ring):
                def put(rows, at, src_c, row, n):
                    sp.dma_start(xs[rows, 2 * ring:2 * ring + 2, :].rearrange("p a n -> p (a n)")[:, at * W:(at + n) * W],
                                 image(x_flat, k, IMT)[:, src_c, bass.ds(row * W, n * W)]
                                 .rearrange("b c n -> c (b n)")).then_inc(x_loaded[ring], 16)
                t = k % IMT
                put(slice(0, C), 0, slice(0, C), t * (2 * SP), 2 * SP)
                for c_to, c_from, nch in ((0, ROLL, C - ROLL), (C - ROLL, 0, ROLL)):
                    rows, src = slice(C + c_to, C + c_to + nch), slice(c_from, c_from + nch)
                    put(rows, 0, src, t * (2 * SP) + ROLL, 2 * SP - ROLL)
                    put(rows, 2 * SP - ROLL, src, (t * (2 * SP) + 2 * SP) % H, ROLL)

            load_pair(0, 0)

            def slot(s):
                ahead = s.n + 5
                if ahead % TSLOT == 0 and (s.turn is not None or ahead // TSLOT < N_TILE):
                    r = ahead // TSLOT
                    k = r if s.turn is None else s.turn * 2 + r
                    if s.turn is not None or r >= 2:
                        wait_alone(sp, q_made, (k - 1) * 2)
                    load_pair(k, r % 2)
                if st := s.strip("store_z"):
                    k, r = st
                    wait_alone(sp, fin_made, k + 1)
                    here = bass.ds((k % STRIPS) * SPX, SPX)
                    def put(roll, m, q0, q1, part):
                        sp.dma_start(image(z_cols[roll], k, STRIPS)[:, m, q0:q1, :, here]
                                     .rearrange("b q y n -> q y (b n)"), fin[part:part + 2 * (q1 - q0), r % 2, :])\
                            .then_inc(z_stored[r % 2], 16)
                    for b in range(2):
                        put(0, b, 0, 16, 64 * b)
                    put(1, 1, 0, 16, 32)
                    for half in range(2):
                        put(1, 0, half * 8 + 1, half * 8 + 8, 96 + half * 16)
                        put(1, 0, half * 8, half * 8 + 1, 96 + half * 16 + 14)
                if ti := s.tile("load_tile"):
                    k, r = ti
                    if s.turn is None:
                        last = min(2 * k + 4, N_STRIP)
                        counts = [(last + 1) // 2, last // 2]
                    else:
                        counts = [k + 2, k + 2]
                    for p in range(2):
                        wait_alone(sp, z_stored[p], counts[p] * (Z_DMAS * 16))
                    if s.later(r, 2):
                        wait_alone(sp, y_made, k - 1)
                    t = (k + 1) % IMT

                    def put(dst, rows, at, src, row, n):
                        sp.dma_start(dst[rows, r % 2, at * W:(at + n) * W],
                                     image(src, k, IMT)[:, :, bass.ds(row * W, n * W)]
                                     .rearrange("b c n -> c (b n)")).then_inc(tile_loaded[r % 2], 16)
                    for half in range(2):
                        rows = slice(half * C, (half + 1) * C)
                        put(xt, rows, 0, x_flat, t * (2 * SP) + half * SP, SP)
                        put(z0t, rows, 0, z_flat[0], t * (2 * SP) + half * SP, SP)
                    put(z2t, slice(0, C), 0, z_flat[1], (t * (2 * SP) + H - ROLL) % H, ROLL)
                    put(z2t, slice(0, C), ROLL, z_flat[1], t * (2 * SP), SP - ROLL)
                    put(z2t, slice(C, 2 * C), 0, z_flat[1], t * (2 * SP) + SP - ROLL, SP)
                if ti := s.tile("tile_out"):
                    k, r = ti
                    wait_alone(sp, y_out_made, k + 1)
                    t = (k + 1) % IMT
                    for half in range(2):
                        sp.dma_start(image(out_flat, k, IMT)[:, :, bass.ds((t * (2 * SP) + half * SP) * W, SPX)]
                                     .rearrange("b c n -> c (b n)"), y_out[half * C:(half + 1) * C, r % 2, :])\
                            .then_inc(out_stored[r % 2], 16)

            pipeline(sp, slot)
            for p in range(2):
                sp.wait_ge(out_stored[p], N_TILE // 2 * 32)

        @block.gpsimd
        def _(pool):
            G = nc.gpsimd
            for buf in (wqkv[:, :, :].rearrange("p a b -> p (a b)"), router_sb[:, :],
                        expert_sb[:, :, :].rearrange("p a b -> p (a b)"), ebias_sb[:, :]):
                G.memset(buf, 0.0).then_inc(const_step, 1)
            pool.wait_ge(const_step, 4)
            pool.sem_inc(weights_cleared, 1)
            pool.wait_ge(const_loaded, 16 * N_WEIGHT_DMAS)

            def spread(dst, src, mask):
                shape = [128, UW, 8, TOK]
                return G.tensor_tensor(dst.rearrange("p n (k i) -> p n k i", i=TOK),
                                       src.rearrange("p (n i) -> p n i", i=TOK).unsqueeze(2).broadcast_to(shape),
                                       mask.unsqueeze(1).unsqueeze(3).broadcast_to(shape), ALU.mult)

            def slot(s):
                if u := s.unit("mask_q"):
                    n, r = u
                    k, kr, j = s.in_strip("mask_q")
                    pool.wait_ge(q_saved, k + 1)
                    if s.later(r, 2):
                        pool.wait_ge(score_made, n - 1)
                    spread(qx[:, r % 2, :, :], q_sb[:, kr % 2, j * UPX:(j + 1) * UPX], const("mask_q")).then_inc(qx_made, 1)
                if u := s.unit("mask_v"):
                    n, r = u
                    k, kr, j = s.in_strip("mask_v")
                    pool.wait_ge(v_copied, k + 1)
                    if s.later(r, 2):
                        pool.wait_ge(vT_made, (n - 1) * 2)
                    spread(vx[:, r % 2, :, :], v_sb[:, kr % 2, j * UPX:(j + 1) * UPX], const("mask_v")).then_inc(vx_made, 1)
                if u := s.unit("total"):
                    n, r = u
                    pool.wait_ge(inv_made, n + 1)
                    pv = per_row(prob[:, r % 4, :])
                    G.tensor_tensor(pv, pv, over_keys(row_inv[:, r % 2, :]), ALU.mult).then_inc(prob_made, 1)
                if st := s.in_strip("pool_taps"):
                    k, kr, j = st
                    if j:
                        pool.wait_ge(tap_made, k * POOL_TAPS + (j + 1))
                        if j > 1:
                            pool.wait_ge(pool_lepe_made, k * (POOL_TAPS - 1) + (j - 1))
                        G.tensor_tensor(lepe_p[:, kr % 2, :], lepe_p[:, kr % 2, :], tap_sb[:, j - 1, :],
                                        ALU.add).then_inc(pool_lepe_made, 1)

            pipeline(pool, slot)

        @block.tensor
        def _(pe):
            pe.wait_ge(const_loaded, 16 * N_WEIGHT_DMAS)
            pe.wait_ge(const_made, N_CONST_MADE)
            nc.tensor.transpose(bank_t[:, 0:KEYS], bias_sb[:, :, :].rearrange("p g a -> p (g a)"),
                                const("ident", KEYS)[:, 0:KEYS]).then_inc(bias_turned, 1)
            for p in range(2):
                MM(bank_s[p][:, :], const("ident"), const_sb[:, 0:UK], start=True, stop=True).then_inc(bias_turned, 1)

            def turn_half(u, t):
                n, r = u
                pe.wait_ge(vx_made, n + 1)
                if t or r > 0:
                    pe.wait_ge(vt_saved, n * 2 + t)
                for w in range(4):
                    last = nc.tensor.transpose(bank_t[:, w * 128:(w + 1) * 128], vx[:, r % 2, 4 * t + w, :], const("ident"))
                last.then_inc(vT_made, 1)

            def slot(s):
                ex = s.in_tile("experts")

                def spread_gate(k, r, e):
                    if r * E + e >= 1:
                        pe.wait_ge(gx_made, k * E + e)
                    MM(bank_g[:, 0:SPX], expert_sel[:, e, :], gateT[:, r % 2, :], start=True, stop=True)\
                        .then_inc(gate_spread, 1)

                def expert(place):
                    e = ex and EXPERT_AT.get((ex[2], place))
                    if e is None:
                        return
                    k, r, _ = ex
                    pe.wait_ge(gx_made, k * E + (e + 1))
                    MM(bank_f[:, 0:SPX], expert_sb[:, e, :], gx[:, e % 2, :], start=False, stop=(e == E - 1))\
                        .then_inc(expert_made, 1)
                    if e + 1 < E:
                        spread_gate(k, r, e + 1)

                if u := s.unit("score"):
                    n, r = u
                    k, kr, j = s.in_strip("score")
                    pe.wait_ge(kx_made, k * 4 + 4)
                    pe.wait_ge(qx_made, n + 1)
                    pe.wait_ge(bias_placed, n + 1)
                    for w in range(UW):
                        last = MM(bank_s[r % 2][:, w * KEYS:(w + 1) * KEYS], qx[:, r % 2, w, :],
                                  kx[:, kr % 2, j * UW + w, :], start=False, stop=(w == UW - 1),
                                  skip_group_check=True)
                    last.then_inc(score_made, 1)
                if u := s.unit("turn_v"):
                    turn_half(u, 0)
                if ti := s.tile("turn_gates"):
                    k, r = ti
                    pe.wait_ge(q_saved, strips_to(s, 2 * k + 11))
                    pe.wait_ge(sq_made, strips_to(s, 2 * k + 12))
                    pe.wait_ge(gates_made, k + 1)
                    for blk in range(TBLK):
                        last = MM(bank_p[0][0:3 * GE, blk * 128:(blk + 1) * 128],
                                  gate_part[:, blk, :, :].rearrange("p a b -> p (a b)"), ident_bf[:, :],
                                  start=True, stop=True)
                    last.then_inc(gateT_made, 1)
                expert(0)
                if st := s.strip("variance"):
                    k, r = st
                    pe.wait_ge(sq_made, k + 1)
                    if ti := s.tile("tile_variance"):
                        pe.wait_ge(fsq_made, ti[0] + 1)
                    if s.later(r, 1):
                        pe.wait_ge(kx_made, k * 4)
                    MM(bank_p[1][:, 0:SPX], const("mean"), sq[:, r % 2, :], start=True, stop=True).then_inc(var_made, 1)
                if st := s.strip("value"):
                    k, r = st
                    pe.wait_ge(xn_made, k + 1)
                    if ti := s.tile("router"):
                        pe.wait_ge(fln_made, ti[0] + 1)
                    MM(bank_p[0][:, 0:SPX], wv[:, :], xs[:, r % 4, :], start=True, stop=True).then_inc(v_made, 1)
                if st := s.strip("query_key"):
                    k, r = st
                    if ti := s.tile("logits"):
                        pe.wait_ge(logitT_saved, ti[0] + 1)
                    pe.wait_ge(xn_made, k + 1)
                    pe.wait_ge(ln_made, k + 1)
                    MM(bank_p[1][:, 0:SPX], wqkv[:, 1, :], xs[:, r % 4, :], start=True, stop=True).then_inc(k_made, 1)
                if u := s.unit("turn_v"):
                    turn_half(u, 1)
                if st := s.strip("query_key"):
                    k, r = st
                    pe.wait_ge(xn_made, k + 1)
                    pe.wait_ge(v_saved, k + 1)
                    MM(bank_p[0][:, 0:SPX], wqkv[:, 0, :], xs[:, r % 4, :], start=True, stop=True).then_inc(q_made, 1)
                expert(1)
                if ti := s.tile("logits"):
                    k, r = ti
                    u = s.unit("product")
                    pe.wait_ge(picked, u[0] * 2 if u else N_UNIT * 2)
                    wait_alone(pe, logitT_saved, k + 1)
                    for blk in range(TBLK):
                        last = nc.tensor.transpose(bank_o[:, LOGITS_AT + blk * GE:LOGITS_AT + (blk + 1) * GE],
                                                   logitT[:, blk * 128:(blk + 1) * 128], const("ident", GE)[:, 0:GE])
                    last.then_inc(logit_made, 1)
                if u := s.unit("product"):
                    n, r = u
                    pe.wait_ge(probT_made, n + 1)
                    pe.wait_ge(vt_saved, (n + 1) * 2)
                    if s.later(r, 1):
                        pe.wait_ge(picked, n * 2)
                    if ti := s.tile("gates"):
                        pe.wait_ge(logit_saved, ti[0] + 1)
                    for w in range(UW):
                        for b in range(2):
                            last = MM(bank_o[64 * b:64 * b + 64, w * 32:(w + 1) * 32], vt[:, r % 2, w, 64 * b:64 * b + 64],
                                      probT[:, r % 2, w, b * 32:(b + 1) * 32], start=True, stop=True)
                    last.then_inc(pv_made, 1)
                if st := s.strip("centre"):
                    k, r = st
                    pe.wait_ge(x_loaded[r // 2 % 2], (k // 4 + 1) * (X_DMAS * 16))
                    if s.later(r, 1):
                        pe.wait_ge(q_saved, k)
                    MM(bank_p[0][:, 0:SPX], const("centre"), xs[:, r % 4, :], start=True, stop=True).then_inc(xc_made, 1)
                if ti := s.tile("tile_sum"):
                    k, r = ti
                    pe.wait_ge(y_made, k + 1)
                    pe.wait_ge(kx_made, strips_to(s, 2 * k + 9) * 4)
                    MM(bank_p[1][:, 0:SPX], const("centre"), y[:, r % 2, :], start=True, stop=True).then_inc(fc_made, 1)
                if ti := s.tile("tile_variance"):
                    k, r = ti
                    pe.wait_ge(fsq_made, k + 1)
                    pe.wait_ge(q_saved, strips_to(s, 2 * k + 9))
                    pe.wait_ge(sq_made, strips_to(s, 2 * k + 10))
                    if ti := s.tile("turn_gates"):
                        pe.wait_ge(gateT_saved, ti[0] + 1)
                    MM(bank_p[0][:, 0:SPX], const("mean"), ysq[:, :], start=True, stop=True).then_inc(fvar_made, 1)
                if ti := s.tile("router"):
                    k, r = ti
                    pe.wait_ge(yn_made, k + 1)
                    pe.wait_ge(ln_made, strips_to(s, 2 * k + 10))
                    MM(bank_p[1][0:GE, 0:SPX], router_sb[:, :], yn[:, r % 2, :], start=True, stop=True)\
                        .then_inc(logitT_made, 1)
                if ti := s.tile("turn_gates"):
                    k, r = ti
                    pe.wait_ge(gateT_saved, k + 1)
                    if s.later(r, 1):
                        pe.wait_ge(y_out_made, k)
                    for part in range(3):
                        MM(bank_f[:, 0:SPX], ebias_part[:, part, :], gateT[:, r % 2, :], start=(part == 0), stop=False)
                    spread_gate(k, r, 0)

            pipeline(pe, slot)

        @block.scalar
        def _(act):
            S = nc.scalar
            S.preload_act_table_set("natural_log_exp_and_others")
            act.wait_ge(const_loaded, 16 * N_WEIGHT_DMAS)
            S.activation(expert_sel[:, :, :].rearrange("p e n -> p (e n)"), const("expert_sel", 3 * GE),
                         ACT.Copy).then_inc(const_made, 1)
            S.activation(ident_bf[:, :], const("ident"), ACT.Copy).then_inc(const_made, 1)
            act.wait_ge(const_made, N_CONST_MADE)
            act.wait_ge(bias_turned, 3)
            S.activation(bias_tile[:, :, :], bank_t[:, 0:KEYS].unsqueeze(1).broadcast_to([128, UW, KEYS]),
                         ACT.Copy).then_inc(bias_made, 1)
            act.wait_ge(bias_made, 1)

            def save_vt(u, t):
                n, r = u
                act.wait_ge(vT_made, n * 2 + (t + 1))
                S.activation(vt[:, r % 2, 4 * t:4 * t + 4, :].rearrange("p n k -> p (n k)"), bank_t[:, :],
                             ACT.Copy).then_inc(vt_saved, 1)

            def slot(s):
                if ti := s.tile("gap_exp"):
                    act.wait_ge(gap_made, ti[0] + 1)
                    S.activation(gate_vec[:, 2, :], gate_vec[:, 2, :], ACT.Exp).then_inc(gap_exp, 1)
                if u := s.unit("turn_v"):
                    save_vt(u, 0)
                if ti := s.tile("turn_gates"):
                    k, r = ti
                    act.wait_ge(gateT_made, k + 1)
                    S.activation(gateT[:, r % 2, :], bank_p[0][0:3 * GE, 0:SPX], ACT.Copy).then_inc(gateT_saved, 1)
                if st := s.strip("variance"):
                    k, r = st
                    act.wait_ge(var_made, k + 1)
                    S.activation(rstd[:, r % 2, :], bank_p[1][:, 0:SPX], ACT.Ln, bias=const("eps1")).then_inc(ln_made, 1)
                    act.wait_ge(ln_made, k + 1)
                    S.activation(rstd[:, r % 2, :], rstd[:, r % 2, :], ACT.Exp, scale=-0.5).then_inc(rstd_made, 1)
                if st := s.strip("value"):
                    k, r = st
                    act.wait_ge(v_made, k + 1)
                    S.activation(vrows(k, 0, 0), bank_p[0][:, 0:SPX].rearrange("p (r w) -> p r w", w=W),
                                 ACT.Copy).then_inc(v_saved, 1)
                if u := s.unit("shift"):
                    n, r = u
                    act.wait_ge(shifted, n + 1)
                    S.activation(prob[:, r % 4, :], prob[:, r % 4, :], ACT.Exp).then_inc(exp_made, 1)
                if u := s.unit("place_bias"):
                    n, r = u
                    if s.later(r, 2):
                        act.wait_ge(shifted, n - 1)
                    S.activation(bank_s[r % 2][:, :], bias_tile[:, :, :].rearrange("p n k -> p (n k)"),
                                 ACT.Copy).then_inc(bias_placed, 1)
                if u := s.unit("turn_v"):
                    save_vt(u, 1)
                if st := s.strip("query_key"):
                    k, r = st
                    act.wait_ge(q_made, k + 1)
                    S.activation(by_window(q_sb[:, r % 2, :]), windows(bank_p[0][:, 0:SPX]), ACT.Copy,
                                 scale=float(HD) ** -0.5).then_inc(q_saved, 1)
                if st := s.strip("query_key"):
                    k, r = st
                    act.wait_ge(k_made, k + 1)
                    for m in range(4):
                        S.activation(kx[:, r % 2, :, m * TOK:(m + 1) * TOK].rearrange("p n (r w) -> p n r w", w=SP),
                                     windows(bank_p[1][:, 0:SPX]), ACT.Copy,
                                     scale=const("mask_k")[:, m:m + 1]).then_inc(kx_made, 1)
                if st := s.strip("centre"):
                    k, r = st
                    act.wait_ge(xc_made, k + 1)
                    S.activation(xs[:, r % 4, :], bank_p[0][:, 0:SPX], ACT.Copy).then_inc(xc_saved, 1)
                    S.activation(sq[:, r % 2, :], bank_p[0][:, 0:SPX], ACT.Square).then_inc(sq_made, 1)
                if st := s.strip("copy_v"):
                    k, r = st
                    S.activation(by_window(v_sb[:, r % 2, :]),
                                 vrows(k, 0, 0).rearrange("p r (n w) -> p n r w", w=SP), ACT.Copy).then_inc(v_copied, 1)
                if st := s.in_strip("tap_products"):
                    k, r, j = st
                    if j == 0 and s.later(r, 2):
                        act.wait_ge(lepe_step, (k - 2) * (9 - POOL_TAPS) + 1)
                    elif j and r:
                        act.wait_ge(pool_lepe_made, (k - 1) * (POOL_TAPS - 1) + j)
                    product = tap_sb[:, j - 1, :] if j else lepe_p[:, r % 2, :]
                    S.activation(product.rearrange("p (r w) -> p r w", w=W), vrows(k, -1, j - 1), ACT.Copy,
                                 scale=lepe_sb[:, j:j + 1]).then_inc(tap_made, 1)
                if ti := s.tile("tile_sum"):
                    k, r = ti
                    act.wait_ge(fc_made, k + 1)
                    S.activation(yn[:, r % 2, :], bank_p[1][:, 0:SPX], ACT.Copy).then_inc(fc_saved, 1)
                    S.activation(ysq[:, :], bank_p[1][:, 0:SPX], ACT.Square).then_inc(fsq_made, 1)
                if ti := s.tile("tile_variance"):
                    k, r = ti
                    act.wait_ge(fvar_made, k + 1)
                    S.activation(yrstd[:, :], bank_p[0][:, 0:SPX], ACT.Ln, bias=const("eps2")).then_inc(fln_made, 1)
                    act.wait_ge(fln_made, k + 1)
                    S.activation(yrstd[:, :], yrstd[:, :], ACT.Exp, scale=-0.5).then_inc(frstd_made, 1)
                if ti := s.tile("router"):
                    k, r = ti
                    act.wait_ge(logitT_made, k + 1)
                    S.activation(logitT[:, :], bank_p[1][0:GE, 0:SPX], ACT.Identity,
                                 bias=router_bias[:, :]).then_inc(logitT_saved, 1)
            pipeline(act, slot)

        @block.vector
        def _(dve):
            V = nc.vector
            V.memset(vpad[:, :], 0.0).then_inc(const_made, 1)
            dve.wait_ge(const_loaded, 16 * N_WEIGHT_DMAS)
            step = [4]

            def chained(ins):
                step[0] += 1
                ins.then_inc(const_step, 1)
                dve.wait_ge(const_step, step[0])

            for b in range(2):
                last = V.tensor_copy(wv[:, 64 * b:64 * b + 64].rearrange("p (q y) -> p q y", y=2),
                                     wqkv[:, 2, :].rearrange("p (q m y) -> p q m y", m=2, y=2)[:, :, b, :])
            last.then_inc(const_made, 1)
            by_head = bias_all[:, :, :].rearrange("p i (A m) -> p (i A) m", A=2)
            chained(V.tensor_tensor(by_head, by_head, const("mask_b", KEYS).unsqueeze(1).broadcast_to([KEYS, 2 * TOK, 4]),
                                    ALU.mult))
            chained(V.tensor_reduce(bias_sb[:, 0, :].rearrange("p (A i) -> p i A", A=2),
                                    bias_all[:, :, :].rearrange("p i (A m) -> p i A m", A=2), AX.X, ALU.add))
            for g in range(1, 4):
                chained(V.tensor_copy(bias_sb[:, g, :], bias_sb[:, 0, :]))
            dve.sem_inc(const_made, 1)
            whole = ebias_sb[:, :]
            for k in range(3):
                chained(V.tensor_copy(ebias_part[:, k, :], whole))
                if k < 2:
                    chained(V.tensor_tensor(ebias_rest[:, k, :], whole, ebias_part[:, k, :], ALU.subtract))
                    whole = ebias_rest[:, k, :]
            dve.sem_inc(const_made, 1)

            GT = TBLK * 2

            def per_e(v):
                return v.rearrange("p (t e) -> p t e", e=E)

            def wide(vec):
                return vec.unsqueeze(2).broadcast_to([128, GT, E])

            def by_block(flat):
                return flat.rearrange("p (t a) -> p t a", a=GE)

            rank = const("rank").unsqueeze(1).broadcast_to([128, GT, E])
            one1, one2, tmp, rest2, gates, left1, left2 = (gate_tmp[:, k, :] for k in range(7))
            best1, best2, gap, vec, total, inv = (gate_vec[:, k, :] for k in range(6))

            def part(k):
                return gate_part[:, :, k, :]

            GATE_SPLIT, GATE_STEPS = 12, 22

            def gate_step_of(k, at):
                if at == 0:
                    dve.wait_ge(logit_saved, k + 1)
                elif at == GATE_SPLIT:
                    dve.wait_ge(gap_exp, k + 1)
                else:
                    dve.wait_ge(gate_step, k * (GATE_STEPS - 2) + (at if at < GATE_SPLIT else at - 1))
                best, src, hot = (best1, logits[:, :], one1) if at < 6 else (best2, rest2, one2)
                choice = at if at < 5 else at - 6
                if choice == 0:
                    done = V.tensor_reduce(best, per_e(src), AX.X, ALU.max)
                elif choice == 1:
                    done = V.tensor_tensor(per_e(tmp), per_e(src), wide(best), ALU.is_equal)
                elif choice == 2:
                    done = V.tensor_tensor(per_e(tmp), per_e(tmp), rank, ALU.mult)
                elif choice == 3:
                    done = V.tensor_reduce(vec, per_e(tmp), AX.X, ALU.max)
                elif choice == 4:
                    done = V.tensor_tensor(per_e(hot), per_e(tmp), wide(vec), ALU.is_equal)
                elif at == 5:
                    done = V.scalar_tensor_tensor(rest2, one1, -3.0e38, logits[:, :], ALU.mult, ALU.add)
                elif at == 11:
                    done = V.tensor_tensor(gap, best2, best1, ALU.subtract)
                elif at == 12:
                    done = V.tensor_scalar(total, gap, 1.0, None, ALU.add)
                elif at == 13:
                    done = V.reciprocal(inv, total)
                elif at == 14:
                    done = V.tensor_tensor(per_e(gates), per_e(one2), wide(gap), ALU.mult)
                elif at == 15:
                    done = V.tensor_tensor(gates, gates, one1, ALU.add)
                elif at == 16:
                    done = V.tensor_tensor(per_e(gates), per_e(gates), wide(inv), ALU.mult)
                elif at == 17:
                    done = V.tensor_copy(part(0), by_block(gates))
                elif at == 18:
                    done = V.tensor_tensor(by_block(left1), by_block(gates), part(0), ALU.subtract)
                elif at == 19:
                    done = V.tensor_copy(part(1), by_block(left1))
                elif at == 20:
                    done = V.tensor_tensor(by_block(left2), by_block(left1), part(1), ALU.subtract)
                else:
                    done = V.tensor_copy(part(2), by_block(left2))
                done.then_inc(gap_made if at == 11 else gates_made if at == 21 else gate_step, 1)

            def slot(s):
                ti = s.tile("gates")
                working = s.in_tile("gates")

                def gate_work(*steps):
                    if working and working[2] < 3:
                        for at in range(*steps[working[2]]):
                            gate_step_of(working[0], at)

                ex = s.in_tile("experts")

                def gate_product(place):
                    e = ex and EXPERT_AT.get((ex[2], place))
                    if e is None:
                        return
                    k, r, _ = ex
                    dve.wait_ge(gate_spread, k * E + (e + 1))
                    if r * E + e >= 2:
                        dve.wait_ge(expert_made, k * E + e - 1)
                    V.tensor_tensor(gx[:, e % 2, :], bank_g[:, 0:SPX], yn[:, r % 2, :], ALU.mult).then_inc(gx_made, 1)

                def tap(k, r, j):
                    acc = lepe[:, r % 2, :].rearrange("p (r w) -> p r w", w=W)
                    first = lepe_p[:, r % 2, :].rearrange("p (r w) -> p r w", w=W)
                    if j == 0:
                        dve.wait_ge(v_saved, strips_to(s, k + 2))
                        dve.wait_ge(pool_lepe_made, (k + 1) * (POOL_TAPS - 1))
                    else:
                        dve.wait_ge(lepe_step, k * (9 - POOL_TAPS) + j)
                    t = POOL_TAPS + j
                    V.scalar_tensor_tensor(acc, vrows(k, t // 3 - 1, t % 3 - 1), lepe_sb[:, t:t + 1],
                                           first if j == 0 else acc, ALU.mult, ALU.add).then_inc(lepe_step, 1)

                shift = s.unit("shift")
                if shift:
                    n, r = shift
                    dve.wait_ge(score_made, n + 1)
                    V.tensor_reduce(row_max[:, r % 2, :], per_row(bank_s[r % 2][:, :]), AX.X, ALU.max).then_inc(max_made, 1)
                gate_product(0)
                gate_work((0, 0), (6, 7), (0, 0))
                if yt := s.tile("tile_out"):
                    k, r = yt
                    dve.wait_ge(expert_made, (k + 1) * E)
                    if s.later(r, 2):
                        dve.wait_ge(out_stored[r % 2], k // 2 * 32)
                    V.tensor_tensor(y_out[:, r % 2, :], bank_f[:, 0:SPX], y[:, r % 2, :], ALU.add).then_inc(y_out_made, 1)
                if shift:
                    n, r = shift
                    dve.wait_ge(max_made, n + 1)
                    V.tensor_tensor(per_row(prob[:, r % 4, :]), per_row(bank_s[r % 2][:, :]),
                                    over_keys(row_max[:, r % 2, :]), ALU.subtract).then_inc(shifted, 1)
                gate_work((0, 0), (7, 8), (12, 13))
                pick = s.unit("pick")
                if pick:
                    n, r = pick
                    k, kr, j = s.in_strip("pick")
                    dve.wait_ge(pv_made, n + 1)
                    pv = bank_o[:, 0:UW * 32].rearrange("p (n m i) -> p m n i", m=2, i=TOK)
                    acc = att[:, kr % 2, j * UPX:(j + 1) * UPX].rearrange("p (n i) -> p n i", i=TOK)
                    V.tensor_scalar(acc, pv[:, 0], const("mask_o")[:, 0:1], None, ALU.mult).then_inc(picked, 1)
                gate_work((0, 0), (0, 0), (13, 14))
                total_of = s.unit("total")
                if total_of:
                    n, r = total_of
                    dve.wait_ge(exp_made, n + 1)
                    V.tensor_reduce(row_sum[:, r % 2, :], per_row(prob[:, r % 4, :]), AX.X, ALU.add).then_inc(sum_made, 1)
                if pick:
                    dve.wait_ge(picked, pick[0] * 2 + 1)
                    V.scalar_tensor_tensor(acc, pv[:, 1], const("mask_o")[:, 1:2], acc, ALU.mult, ALU.add).then_inc(picked, 1)
                if yt := s.tile("tile_sum"):
                    k, r = yt
                    dve.wait_ge(tile_loaded[r % 2], (k // 2 + 1) * (TILE_DMAS * 16))
                    if s.later(r, 2):
                        dve.wait_ge(y_out_made, k - 1)
                    V.tensor_tensor(y[:, r % 2, :], xt[:, r % 2, :], z0t[:, r % 2, :], ALU.add).then_inc(y_step, 1)
                if yt := s.tile("router"):
                    k, r = yt
                    dve.wait_ge(frstd_made, k + 1)
                    V.tensor_tensor(yn[:, r % 2, :], yn[:, r % 2, :], yrstd[:, :], ALU.mult).then_inc(yn_made, 1)
                if ti:
                    k, r = ti
                    dve.wait_ge(logit_made, k + 1)
                    V.tensor_copy(logits[:, :], bank_o[:, LOGITS_AT:LOGITS_AT + TBLK * GE]).then_inc(logit_saved, 1)
                gate_work((0, 1), (8, 9), (14, 15))
                if total_of:
                    n, r = total_of
                    dve.wait_ge(sum_made, n + 1)
                    V.reciprocal(row_inv[:, r % 2, :], row_sum[:, r % 2, :]).then_inc(inv_made, 1)
                if yt := s.tile("tile_sum"):
                    k, r = yt
                    dve.wait_ge(y_step, k + 1)
                    V.tensor_tensor(y[:, r % 2, :], y[:, r % 2, :], z2t[:, r % 2, :], ALU.add).then_inc(y_made, 1)
                if st := s.strip("add_taps"):
                    k, r = st
                    if s.later(r, 2):
                        dve.wait_ge(z_stored[r % 2], k // 2 * (Z_DMAS * 16))
                    dve.wait_ge(lepe_step, (k + 1) * (9 - POOL_TAPS))
                    dve.wait_ge(picked, (k + 1) * (2 * UNITS))
                    V.tensor_tensor(windows(fin[:, r % 2, :]), by_window(att[:, r % 2, :]),
                                    windows(lepe[:, r % 2, :]), ALU.add).then_inc(fin_made, 1)
                gate_work((1, 2), (9, 10), (15, 16))
                gate_work((2, 3), (10, 11), (16, 17))
                gate_product(1)
                taps = s.in_strip("taps")
                if taps:
                    tap(taps[0], taps[1], 2 * taps[2])
                gate_work((3, 4), (11, 12), (17, 18))
                if u := s.unit("turn_p"):
                    n, r = u
                    dve.wait_ge(prob_made, n + 1)
                    V.transpose(probT[:, r % 2, :, :].rearrange("p n k -> p (n k)"), prob[:, r % 4, :]).then_inc(probT_made, 1)
                gate_work((4, 5), (0, 0), (18, 20))
                if taps:
                    tap(taps[0], taps[1], 2 * taps[2] + 1)
                if st := s.strip("variance"):
                    k, r = st
                    dve.wait_ge(rstd_made, k + 1)
                    V.tensor_tensor(xs[:, r % 4, :], xs[:, r % 4, :], rstd[:, r % 2, :], ALU.mult).then_inc(xn_made, 1)
                gate_work((5, 6), (0, 0), (20, 22))

            pipeline(dve, slot)


_INS = ["x", "L0_conv_qkv_w", "L0_conv_lepe_w", "L0_conv_bias_table", "L0_ffn_router_w", "L0_ffn_router_b",
        "L0_ffn_expert_w", "L0_ffn_expert_b"]


def kernel(**inputs):
    import numpy as _np
    import concourse.bacc as _bacc
    from concourse import mybir as _mybir
    from concourse.bass_utils import run_bass_kernel_spmd as _run

    nc = _bacc.Bacc("TRN2", target_bir_lowering=False, num_devices=1)
    arrays, args = {}, []
    for name in _INS:
        arrays[f"in_{name}"] = _np.ascontiguousarray(inputs[name])
    arrays["in_constants"] = CONSTS
    for name, a in arrays.items():
        args.append(nc.dram_tensor(name, a.shape, _mybir.dt.from_np(a.dtype), kind="ExternalInput").ap())
    args.append(nc.dram_tensor("out_y", (B, C, H, W), _mybir.dt.float32, kind="ExternalOutput").ap())
    metaformer_block(nc, *args)
    r = _run(nc, [arrays], core_ids=[0])
    return r.results[0]["out_y"]
```
